# Optimizing a Trainium2 kernel written in Bass

```python
import numpy as np
import jax
import jax.numpy as jnp

def _softmax(x, axis=-1):
    return jax.nn.softmax(x, axis=axis)

def _gelu(x):
    return jax.nn.gelu(x, approximate=True)

def _silu(x):
    return jax.nn.silu(x)

def _sigmoid(x):
    return jax.nn.sigmoid(x)

def _layernorm(x, axis=-1, eps=1e-05):
    m = jnp.mean(x, axis=axis, keepdims=True)
    v = jnp.var(x, axis=axis, keepdims=True)
    return (x - m) / jnp.sqrt(v + eps)

def _scatter_add(tgt, idx, src, axis=0):
    return tgt.at[idx].add(src)

def _segment_sum(src, seg, n):
    return jax.ops.segment_sum(src, seg, n)
kernel_name = 'mk_adj_preln_d4_adj_r2_6491fc'

def setup_inputs(seed: int=0):
    np.random.seed(seed)
    _w = jnp.asarray

    def _rec_inputs():
        import jax
        import jax.numpy as jnp
        _gk = jax.random.key(seed)
        x = -8.015e-05 + 0.9999 * jax.random.normal(jax.random.fold_in(_gk, 1), (8, 1024, 128), jnp.float32)
        _w = (1.0 + jnp.arange(1024, dtype=jnp.float32)) ** (-0.5)
        _w = _w / _w.mean()
        _pij = jnp.clip(0.00195312 * _w[:, None] * _w[None, :], 0.0, 1.0)
        _a = jax.random.uniform(jax.random.fold_in(_gk, 2), (8, 1024, 1024)) < _pij
        _a = jnp.logical_or(_a, jnp.swapaxes(_a, -1, -2))
        _a = jnp.logical_or(_a, jnp.eye(1024, dtype=bool))
        _af = _a.astype(jnp.float32)
        _af = _af * jax.random.uniform(jax.random.fold_in(_gk, 3), (8, 1024, 1024), jnp.float32, 0.05, 0.999837)
        adj = _af
        return (x, adj)
    x, adj = _rec_inputs()

    def _L0_gnn_setup():
        import jax, jax.numpy as jnp
        import numpy as np
        GROUPS = [list(range(25)), [0, 1, 2, 3, 4, 5, 6, 7, 8], [0, 9, 10, 11, 12, 13, 14], [6, 7, 8, 12, 13, 14], [3, 4, 5, 9, 10, 11]]
        B, N, D_IN, D_HID = (4096, 25, 128, 256)

        def _graph_conv(x, adj, W, b):
            n = adj.shape[-1]
            A = adj + jnp.eye(n, dtype=adj.dtype)
            deg = jnp.sum(A, axis=-1)
            deg_safe = jnp.where(deg == 0, 1.0, deg)
            dinv = jnp.where(deg == 0, 0.0, deg_safe ** (-0.5))
            norm_adj = dinv[:, :, None] * A * dinv[:, None, :]
            support = jnp.einsum('bnd,de->bne', x, W)
            out = jnp.einsum('bnm,bme->bne', norm_adj, support) + b
            return jax.nn.relu(out)
        key = jax.random.key(seed)
        ks = jax.random.split(key, 7)
        s1 = float(np.sqrt(6.0 / (D_IN + D_HID)))
        s2 = float(np.sqrt(6.0 / (D_HID + D_IN)))
        return {'x': jax.random.normal(ks[0], (B, N, D_IN), dtype=jnp.float32), 'adj': jax.random.uniform(ks[1], (B, N, N), dtype=jnp.float32), 'W1': jax.random.uniform(ks[2], (5, D_IN, D_HID), jnp.float32, -s1, s1), 'b1': jnp.zeros((5, D_HID), dtype=jnp.float32), 'W2': jax.random.uniform(ks[3], (5, D_HID, D_IN), jnp.float32, -s2, s2), 'b2': jnp.zeros((5, D_IN), dtype=jnp.float32), 'fusion_w': jnp.ones((5,), dtype=jnp.float32)}
    _L0_gnn_all = _L0_gnn_setup()
    _L0_gnn_in = {k: v for k, v in _L0_gnn_all.items() if k in ('W1', 'b1', 'W2', 'b2', 'fusion_w')}
    del _L0_gnn_all

    def _L1_gnn_setup():
        import jax, jax.numpy as jnp
        import numpy as np
        B, N, D, H = (8, 1024, 128, 512)
        RMS_EPS = 1e-06

        def _rmsnorm(h, w, eps=RMS_EPS):
            var = jnp.mean(jnp.square(h), axis=-1, keepdims=True)
            return h * jax.lax.rsqrt(var + eps) * w
        key = jax.random.key(seed)
        ks = jax.random.split(key, 5)
        x = jax.random.normal(ks[0], (B, N, D), dtype=jnp.float32)
        adjacency = jax.random.uniform(ks[1], (B, N, N), dtype=jnp.float32)
        epsilon = jnp.zeros((), dtype=jnp.float32)
        W1 = jax.random.normal(ks[2], (D, H), dtype=jnp.float32) * (1.0 / np.sqrt(D))
        b1 = jnp.zeros((H,), dtype=jnp.float32)
        rms_weight = jnp.ones((H,), dtype=jnp.float32)
        W2 = jax.random.normal(ks[3], (H, D), dtype=jnp.float32) * (1.0 / np.sqrt(H))
        b2 = jnp.zeros((D,), dtype=jnp.float32)
        return {'x': x, 'adjacency': adjacency, 'epsilon': epsilon, 'W1': W1, 'b1': b1, 'rms_weight': rms_weight, 'W2': W2, 'b2': b2}
    _L1_gnn_all = _L1_gnn_setup()
    _L1_gnn_in = {k: v for k, v in _L1_gnn_all.items() if k in ('epsilon', 'W1', 'b1', 'rms_weight', 'W2', 'b2')}
    del _L1_gnn_all

    def _L2_gnn_setup():
        import jax, jax.numpy as jnp
        import numpy as np
        LN_EPS = 1e-05
        key = jax.random.key(seed)
        k1, k2, k3, k4 = jax.random.split(key, 4)
        B, N, F, O = (8, 1024, 128, 128)
        x = jax.random.normal(k1, (B, N, F), dtype=jnp.float32)
        adj = jax.random.uniform(k2, (B, N, N), dtype=jnp.float32)
        gamma = jnp.ones((F,), jnp.float32)
        beta = jnp.zeros((F,), jnp.float32)
        W_self = jax.random.normal(k3, (F, O), dtype=jnp.float32) * (1.0 / np.sqrt(F))
        W_neigh = jax.random.normal(k4, (F, O), dtype=jnp.float32) * (1.0 / np.sqrt(F))
        return {'x': x, 'adj': adj, 'gamma': gamma, 'beta': beta, 'W_self': W_self, 'W_neigh': W_neigh}
    _L2_gnn_all = _L2_gnn_setup()
    _L2_gnn_in = {k: v for k, v in _L2_gnn_all.items() if k in ('gamma', 'beta', 'W_self', 'W_neigh')}
    del _L2_gnn_all

    def _L3_gnn_setup():
        import jax, jax.numpy as jnp
        import numpy as np
        B, N, F_IN, F_OUT = (8, 1024, 128, 128)
        key = jax.random.key(seed)
        k1, k2, k3, k4 = jax.random.split(key, 4)
        node_features = jax.random.normal(k1, (B, N, F_IN), dtype=jnp.float32)
        adj_matrix = jax.random.uniform(k2, (B, N, N), dtype=jnp.float32)
        lim = 1.0 / np.sqrt(F_IN)
        W = jax.random.uniform(k3, (F_OUT, F_IN), minval=-lim, maxval=lim, dtype=jnp.float32)
        b = jax.random.uniform(k4, (F_OUT,), minval=-lim, maxval=lim, dtype=jnp.float32)
        return {'node_features': node_features, 'adj_matrix': adj_matrix, 'W': W, 'b': b}
    _L3_gnn_all = _L3_gnn_setup()
    _L3_gnn_in = {k: v for k, v in _L3_gnn_all.items() if k in ('W', 'b')}
    del _L3_gnn_all
    return {'x': x, 'adj': adj, 'L0_gnn_W1': _L0_gnn_in['W1'], 'L0_gnn_b1': _L0_gnn_in['b1'], 'L0_gnn_W2': _L0_gnn_in['W2'], 'L0_gnn_b2': _L0_gnn_in['b2'], 'L0_gnn_fusion_w': _L0_gnn_in['fusion_w'], 'L1_gnn_epsilon': _L1_gnn_in['epsilon'], 'L1_gnn_W1': _L1_gnn_in['W1'], 'L1_gnn_b1': _L1_gnn_in['b1'], 'L1_gnn_rms_weight': _L1_gnn_in['rms_weight'], 'L1_gnn_W2': _L1_gnn_in['W2'], 'L1_gnn_b2': _L1_gnn_in['b2'], 'L2_gnn_gamma': _L2_gnn_in['gamma'], 'L2_gnn_beta': _L2_gnn_in['beta'], 'L2_gnn_W_self': _L2_gnn_in['W_self'], 'L2_gnn_W_neigh': _L2_gnn_in['W_neigh'], 'L3_gnn_W': _L3_gnn_in['W'], 'L3_gnn_b': _L3_gnn_in['b']}

def reference(x, adj, L0_gnn_W1, L0_gnn_b1, L0_gnn_W2, L0_gnn_b2, L0_gnn_fusion_w, L1_gnn_epsilon, L1_gnn_W1, L1_gnn_b1, L1_gnn_rms_weight, L1_gnn_W2, L1_gnn_b2, L2_gnn_gamma, L2_gnn_beta, L2_gnn_W_self, L2_gnn_W_neigh, L3_gnn_W, L3_gnn_b):
    import jax
    import jax.numpy as jnp

    def _L0_gnn_ref(x, adj, W1, b1, W2, b2, fusion_w):
        import jax, jax.numpy as jnp
        import numpy as np
        GROUPS = [list(range(25)), [0, 1, 2, 3, 4, 5, 6, 7, 8], [0, 9, 10, 11, 12, 13, 14], [6, 7, 8, 12, 13, 14], [3, 4, 5, 9, 10, 11]]
        B, N, D_IN, D_HID = (4096, 25, 128, 256)

        def _graph_conv(x, adj, W, b):
            n = adj.shape[-1]
            A = adj + jnp.eye(n, dtype=adj.dtype)
            deg = jnp.sum(A, axis=-1)
            deg_safe = jnp.where(deg == 0, 1.0, deg)
            dinv = jnp.where(deg == 0, 0.0, deg_safe ** (-0.5))
            norm_adj = dinv[:, :, None] * A * dinv[:, None, :]
            support = jnp.einsum('bnd,de->bne', x, W)
            out = jnp.einsum('bnm,bme->bne', norm_adj, support) + b
            return jax.nn.relu(out)
        norm_w = jax.nn.softmax(fusion_w)
        fused = jnp.zeros_like(x)
        for g, idx_list in enumerate(GROUPS):
            idx = jnp.asarray(idx_list)
            x_g = x[:, idx, :]
            adj_g = adj[:, idx][:, :, idx]
            h = _graph_conv(x_g, adj_g, W1[g], b1[g])
            out_g = _graph_conv(h, adj_g, W2[g], b2[g])
            fused = fused.at[:, idx, :].add(norm_w[g] * out_g)
        return fused

    def _L1_gnn_ref(x, adjacency, epsilon, W1, b1, rms_weight, W2, b2):
        import jax, jax.numpy as jnp
        import numpy as np
        B, N, D, H = (8, 1024, 128, 512)
        RMS_EPS = 1e-06

        def _rmsnorm(h, w, eps=RMS_EPS):
            var = jnp.mean(jnp.square(h), axis=-1, keepdims=True)
            return h * jax.lax.rsqrt(var + eps) * w
        neighbor_sum = jnp.einsum('bnm,bmd->bnd', adjacency, x)
        agg = epsilon * x + neighbor_sum
        h = jnp.einsum('bnd,dh->bnh', agg, W1) + b1
        h = jax.nn.silu(_rmsnorm(h, rms_weight))
        out = jnp.einsum('bnh,hd->bnd', h, W2) + b2
        return out

    def _L2_gnn_ref(x, adj, gamma, beta, W_self, W_neigh):
        import jax, jax.numpy as jnp
        import numpy as np
        LN_EPS = 1e-05
        mu = jnp.mean(x, axis=-1, keepdims=True)
        var = jnp.mean(jnp.square(x - mu), axis=-1, keepdims=True)
        xn = (x - mu) * jax.lax.rsqrt(var + LN_EPS) * gamma + beta
        d_out = jnp.sum(adj, axis=1)
        d_in = jnp.sum(adj, axis=2)
        s_out = jnp.where(d_out != 0, jax.lax.rsqrt(d_out), 0.0)
        s_in = jnp.where(d_in != 0, jax.lax.rsqrt(d_in), 0.0)
        A_norm = s_out[:, :, None] * adj * s_in[:, None, :]
        eye = jnp.eye(adj.shape[1], dtype=adj.dtype)
        L = eye[None, :, :] - A_norm
        neighbor = jnp.einsum('bij,bjf->bif', L, xn)
        pre = xn @ W_self + neighbor @ W_neigh
        return jax.nn.softplus(pre)

    def _L3_gnn_ref(node_features, adj_matrix, W, b):
        import jax, jax.numpy as jnp
        import numpy as np
        B, N, F_IN, F_OUT = (8, 1024, 128, 128)
        degree = jnp.sum(adj_matrix, axis=-1)
        d_inv_sqrt = jnp.power(degree, -0.5)
        d_inv_sqrt = jnp.where(jnp.isinf(d_inv_sqrt), 0.0, d_inv_sqrt)
        norm_adj = adj_matrix * d_inv_sqrt[:, :, None] * d_inv_sqrt[:, None, :]
        transformed = jnp.einsum('bnf,of->bno', node_features, W) + b
        output = jnp.einsum('bnm,bmo->bno', norm_adj, transformed)
        return jax.nn.relu(output)
    h = jnp.maximum(_layernorm(x, axis=-1), 0.0)
    x = x + _L0_gnn_ref(h, adj, L0_gnn_W1, L0_gnn_b1, L0_gnn_W2, L0_gnn_b2, L0_gnn_fusion_w)
    h = jnp.maximum(_layernorm(x, axis=-1), 0.0)
    x = x + _L1_gnn_ref(h, adj, L1_gnn_epsilon, L1_gnn_W1, L1_gnn_b1, L1_gnn_rms_weight, L1_gnn_W2, L1_gnn_b2)
    h = jnp.maximum(_layernorm(x, axis=-1), 0.0)
    x = x + _L2_gnn_ref(h, adj, L2_gnn_gamma, L2_gnn_beta, L2_gnn_W_self, L2_gnn_W_neigh)
    h = jnp.maximum(_layernorm(x, axis=-1), 0.0)
    x = x + _L3_gnn_ref(h, adj, L3_gnn_W, L3_gnn_b)
    return x

_drawn_inputs = setup_inputs


def setup_inputs(seed=0):
    import zlib

    import numpy as np

    out = dict(_drawn_inputs(seed))
    spreads = {'L0_gnn_b1': (0.0, 0.8),
     'L0_gnn_b2': (0.0, 2.0),
     'L0_gnn_fusion_w': (1.0, 0.6),
     'L1_gnn_b1': (0.0, 0.1),
     'L1_gnn_rms_weight': (1.0, 0.2),
     'L1_gnn_b2': (0.0, 0.1),
     'L2_gnn_gamma': (1.0, 0.2),
     'L2_gnn_beta': (0.0, 0.1)}
    factors = {'L0_gnn_W1': 6.155, 'L0_gnn_W2': 5.1, 'L3_gnn_b': 2.673}
    for name, (base, spread) in spreads.items():
        noise = np.random.default_rng([zlib.crc32(name.encode()), seed]).standard_normal(out[name].shape)
        drawn = base * np.exp(spread * noise) if base else spread * noise
        out[name] = jnp.asarray(drawn.astype(out[name].dtype))
    for name, factor in factors.items():
        out[name] = (out[name] * factor).astype(out[name].dtype)
    return out
```

```python
from contextlib import ExitStack

import numpy as np

import concourse.bass as bass
from concourse import mybir

B, N, D, HID = 8, 1024, 128, 512
P = 128
NB = N // P
HB = NB // 2
HALF = N // 2
KH = HID // P
G0, T0, S0 = 5, 2, 32
E0 = 256
N0 = 25
XS = 3
RS = 2
GROUPS = [list(range(25)), [0, 1, 2, 3, 4, 5, 6, 7, 8], [0, 9, 10, 11, 12, 13, 14], [6, 7, 8, 12, 13, 14],
          [3, 4, 5, 9, 10, 11]]

F32 = mybir.dt.float32
F32R = mybir.dt.float32r
ALU = mybir.AluOpType
ACT = mybir.ActivationFunctionType
AX = mybir.AxisListType


def cnt(graph, per_graph, c):
    return graph * per_graph + c


def need(eng, sem, value):
    if isinstance(value, int) and value <= 0:
        return
    eng.wait_ge(sem, value)


def build(nc, t_in, out):
    x_d, adjT_d = t_in["x"], t_in["adjT"]
    x0_d = nc.dram_tensor("x_layer0", (T0, P, D), F32).ap()

    with ExitStack() as ctx:
        def sb(name, shape, dt=F32, where=ctx):
            return where.enter_context(nc.sbuf_tensor(name, shape, dt))

        def sem(name):
            return ctx.enter_context(nc.semaphore(name))

        def bank(name):
            return ctx.enter_context(nc.psum_tensor(name, [P, HALF], F32))

        acc12 = [bank("acc12_0"), bank("acc12_1")]
        acc3 = [bank("acc3_0"), bank("acc3_1")]
        hid = [bank("hid_0"), bank("hid_1")]
        turn = bank("turn")
        mlp = bank("mlp")
        p1_bank = [turn, mlp]

        X = sb("X", [P, XS * N])
        raw = sb("raw", [P, RS, N])
        rowsum = sb("rowsum", [P, N])
        v1H, v1L = sb("v1H", [P, N], F32R), sb("v1L", [P, N], F32R)
        v2H, v2L = sb("v2H", [P, N], F32R), sb("v2L", [P, N], F32R)
        v3H, v3L = sb("v3H", [P, N], F32R), sb("v3L", [P, N], F32R)
        colT = sb("colT", [P, N])
        xn = sb("xn", [P, HALF])
        fT = sb("fT", [P, HALF])
        t = [sb("t_0", [P, HALF]), sb("t_1", [P, HALF])]
        u = sb("u", [P, HALF])
        sT = sb("sT", [P, HALF])
        z = [sT, u]
        w1 = sb("w1", [P, HID])
        w2 = sb("w2", [P, HID])
        wneigh = sb("wneigh", [P, D])
        wsum = sb("wsum", [P, D])
        w3 = sb("w3", [P, D])
        ident = sb("ident", [P, P])
        epsH, epsL = sb("epsH", [P, P], F32R), sb("epsL", [P, P], F32R)
        wrms = sb("wrms", [P, HID])
        b2bc, gam, bet, b3bc = sb("b2bc", [P, D]), sb("gam", [P, D]), sb("bet", [P, D]), sb("b3bc", [P, D])
        b1R = sb("b1R", [2, HID], F32R)
        onesR = sb("onesR", [2, P], F32R)
        ones = sb("ones", [P, 1])
        eps = sb("eps", [P, 1])
        power = sb("power", [P, 16])
        stat6 = sb("stat6", [P, HB, 6])
        mv = [sb("mv_0", [P, HB, 2]), sb("mv_1", [P, HB, 2])]
        veps = [sb("veps_0", [P, HB]), sb("veps_1", [P, HB])]
        rstd = [sb("rstd_0", [P, HB]), sb("rstd_1", [P, HB])]
        junk = sb("junk", [P, HID], mybir.dt.bfloat16)
        ss = sb("ss", [P, 2])
        tick = sb("tick", [P, 2])
        rms_eps = sb("rms_eps", [P, 1])
        sse = sb("sse", [P, 2])
        rrms = sb("rrms", [P, 2])
        deg = sb("deg", [P, 16])
        dnz = sb("dnz", [P, 16])
        dz = sb("dz", [P, 16])
        dsafe = sb("dsafe", [P, 16])
        dpow = sb("dpow", [P, 16])
        sc_b = sb("sc_b", [P, 16])
        sc_p = sb("sc_p", [P, 16])

        def sb0(name, shape, dt=F32):
            return sb(name, shape, dt, early)
        with ExitStack() as early:
            xr = sb0("xr", [P, T0, D])
            h0 = sb0("h0", [P, T0, D])
            adj0 = sb0("adj0", [P, T0, P])
            member = sb0("member", [P, G0])
            ma = sb0("ma", [P, T0, G0, P])
            gt1 = sb0("gt1", [P, T0, G0 * P])
            mask0 = sb0("mask0", [P, G0, P])
        adjH = sb("adjH", [P, 2 * NB * N], F32R)
        with ExitStack() as early:
            w10 = sb0("w10", [P, G0, E0])
            w20 = sb0("w20", [P, G0, 2, D])
            b10 = sb0("b10", [P, G0 * E0])
            b20 = sb0("b20", [P, G0 * D])
            h10 = sb0("h10", [P, 2, E0])
            gt2 = sb0("gt2", [P, 2, E0])
            o0 = sb0("o0", [P, 2, D])
            fus = sb0("fus", [P, G0])
            fmx = sb0("fmx", [P, 2])
            fex = sb0("fex", [P, G0])
            fsum = sb0("fsum", [P, 2])
            cw = sb0("cw", [P, G0])
            st0 = sb0("st0", [P, T0, 6])
            mv0 = sb0("mv0", [P, T0, 2])
            ve0 = sb0("ve0", [P, T0])
            rs0 = sb0("rs0", [P, T0])
            dg0 = sb0("dg0", [P, 4, T0 * G0])
            di0 = sb0("di0", [P, T0 * G0])
            wself = sb0("wself", [P, D])
            epsI = sb0("epsI", [P, P])
            b1r2 = sb0("b1r2", [2, HID])
            b1hi = sb0("b1hi", [2, HID], F32R)
            b1lo = sb0("b1lo", [2, HID])
        adjL = sb("adjL", [P, 2 * NB * N], F32R)

        l0_in, l0_w, w_in, const_ready = sem("l0_in"), sem("l0_w"), sem("w_in"), sem("const_ready")
        s0_dve, s0_pool, s0_act = sem("layer0_dve"), sem("layer0_pool"), sem("layer0_act")
        s0_own = sem("layer0_dve_own")
        s0_pe, x0_stored = sem("layer0_pe"), sem("x0_stored")
        c1_mm, g2_mm, out_mm = sem("c1_mm"), sem("g2_mm"), sem("out_mm")
        c1_scaled, c1_relu, g2_copied = sem("c1_scaled"), sem("c1_relu"), sem("g2_copied")
        out_scaled, out_weighted, x0_added = sem("out_scaled"), sem("out_weighted"), sem("x0_added")
        raw_in = [sem(f"raw_in_{s}") for s in range(RS)]
        xm_in, x0_in = sem("x_in"), sem("x_layer0_in")
        hi_ready, lo_ready = sem("hi_ready"), sem("lo_ready")
        summed = sem("summed")
        sc_p_last = sem("sc_p_last")
        rs_mm, deg_steps, deg_pow = sem("rs_mm"), sem("deg_steps"), sem("deg_pow")
        ln = ["ln1", "ln2a", "ln2b", "ln3"]
        ln_steps = {k: sem(k + "_steps") for k in ln}
        ln_rstd = {k: sem(k + "_rstd") for k in ln}
        relu_done = {k: sem(k + "_relu") for k in ("ln1", "ln2a", "ln3")}
        vH = {k: sem(f"v{k}_hi") for k in (1, 2, 3)}
        vL = {k: sem(f"v{k}_lo") for k in (1, 2, 3)}
        xb2 = sem("x_plus_b2")
        a1_mm, a2_mm = sem("a1_mm"), sem("a2_mm")
        a3_tile = sem("a3_tile")
        agg_copied, nb_copied, o_copied = sem("agg_copied"), sem("nb_copied"), sem("o_copied")
        agg_copied2, nb_copied2, o_copied2 = sem("agg_copied2"), sem("nb_copied2"), sem("o_copied2")
        w1_mm, turn_mm, w2_mm = sem("w1_mm"), sem("turn_mm"), sem("w2_mm")
        squared, msq, rms, weighted = sem("squared"), sem("mean_square"), sem("rms"), sem("weighted")
        silu_done, sT_copied, x1_done = sem("silu_done"), sem("sT_copied"), sem("x1_done")
        xn_steps, v2_scaled = sem("xn_steps"), sem("v2_scaled")
        xnT_mm, xnT_copied, p1_mm, p1_copied, p2_mm = (sem(s) for s in ("xnT_mm", "xnT_copied", "p1_mm", "p1_copied", "p2_mm"))
        z_done, xz_done, sp_steps, x2_done = sem("z_done"), sem("x_relu_z"), sem("softplus_steps"), sem("x2_done")
        hT_mm, hT_copied, t3_mm, v3_steps = sem("hT_mm"), sem("hT_copied"), sem("t3_mm"), sem("v3_steps")
        oT_mm, o_scaled, x3_done = sem("oT_mm"), sem("o_scaled"), sem("x3_done")
        stored = [sem("stored_0"), sem("stored_1")]

        def xcols(graph, k0, k):
            return X[:, bass.ds((graph % XS) * N + k0 * D, k * D)]

        def tile_cols(graph, j, c0, c):
            return bass.ds(((graph + 1) % 2) * (NB * N) + j * N + c0, c)

        def blk(ap, k):
            return ap[:, k * D:(k + 1) * D]

        def by_block(ap):
            return ap.rearrange("p (k d) -> p k d", d=D)

        def over_blocks(ap, k=HB):
            return ap[:, :].unsqueeze(1).broadcast_to([P, k, D])

        block = ctx.enter_context(nc.Block())

        @block.sync
        def _(sp):
            def load(c):
                for g in range(2):
                    need(sp, stored[g], cnt(c - XS, 16, 16) if not isinstance(c, int) or c >= XS else 0)
                if isinstance(c, int) and c == 0:
                    load_x(c)
                    load_tiles(c)
                    sp.wait_ge(x0_stored, 16)
                    load_x0(c)
                else:
                    sp.wait_ge(x0_in, cnt(c - 1, 16, 16))
                    load_x(c)
                    load_x0(c)
                    load_tiles(c)

            def load_x(c):
                sp.dma_start(by_block(xcols(c, 0, NB)),
                             x_d[bass.ds(c, 1)].rearrange("a (k p) d -> p (a k) d", p=P)).then_inc(xm_in, 16)

            def load_x0(c):
                sp.wait_ge(xm_in, cnt(c, 16, 16))
                sp.dma_start(xcols(c, 0, 1)[0:N0, :],
                             x0_d.rearrange("t (b n) d -> (t b) n d", n=S0)[bass.ds(c, 1), 0:N0, :]
                             .rearrange("a n d -> (a n) d")).then_inc(x0_in, 16)

            def load_tiles(c):
                for j in range(NB):
                    if j >= RS:
                        sp.wait_ge(summed, cnt(c, 2 * (NB - 1), 2 * max(j - RS, 1)))
                    else:
                        need(sp, summed, cnt(c, 2 * (NB - 1), 2 * (j - RS + 1)) if not isinstance(c, int) or c else 0)
                    sp.dma_start(raw[:, j % RS, :],
                                 adjT_d[bass.ds(c, 1), j * P:(j + 1) * P, :].rearrange("a p n -> p (a n)")
                                 ).then_inc(raw_in[j % RS], 16)

            def store(p):
                for g in range(2):
                    sp.wait_ge(x3_done, cnt(p, 2, g + 1))
                    sp.dma_start(out[bass.ds(p, 1), g * HALF:(g + 1) * HALF, :].rearrange("a (k p) d -> p (a k) d", p=P),
                                 by_block(xcols(p, g * HB, HB))).then_inc(stored[g], 16)

            load(0)
            load(1)
            load(2)
            store(0)
            with sp.Fori(2, B - 1) as i:
                load(i + 1)
                store(i - 1)
            for p in range(B - 2, B):
                store(p)
            for g in range(2):
                sp.wait_ge(stored[g], 16 * B)

        @block.tensor
        def _(pe):
            mm = nc.tensor.matmul

            def layer0():
                pe.wait_ge(const_ready, 1)
                pe.wait_ge(s0_dve, 2)
                for tt in range(T0):
                    for g in range(G0):
                        last = mm(acc12[0][:, tt * G0 + g:tt * G0 + g + 1], ma[:, tt, g, :], ones[:, :],
                                  start=True, stop=True)
                last.then_inc(s0_pe, 1)
                pe.wait_ge(s0_dve, 9)
                pe.wait_ge(s0_act, 2)
                for tt in range(T0):
                    m = ma[:, tt, :, :].rearrange("p g n -> p (g n)")
                    mm(acc3[tt][:, :], h0[:, tt, :], m[:, 0:HALF], start=True, stop=True)
                    last = mm(hid[tt][:, 0:P], h0[:, tt, :], m[:, HALF:], start=True, stop=True)
                last.then_inc(s0_pe, 1)
                pe.wait_ge(l0_w, 16 * 4)
                pe.wait_ge(s0_act, 4)
                Q0 = T0 * G0
                for q in range(Q0 + 2):
                    if q < Q0:
                        tt, g = q // G0, q % G0
                        need(pe, c1_scaled, q - 1)
                        mm(hid[q % 2][:, 0:E0], gt1[:, tt, g * P:(g + 1) * P], w10[:, g, :],
                           start=True, stop=True).then_inc(c1_mm, 1)
                    if 1 <= q <= Q0:
                        r = q - 1
                        tt, g = r // G0, r % G0
                        pe.wait_ge(c1_relu, r + 1)
                        need(pe, g2_copied, r)
                        for c in range(2):
                            last = mm(turn[:, c * P:(c + 1) * P], h10[:, r % 2, c * P:(c + 1) * P],
                                      ma[:, tt, g, :], start=True, stop=True)
                        last.then_inc(g2_mm, 1)
                    if q >= 2:
                        r = q - 2
                        g = r % G0
                        pe.wait_ge(g2_copied, r + 1)
                        need(pe, out_scaled, r)
                        for c in range(2):
                            last = mm(mlp[:, 0:D], gt2[:, r % 2, c * P:(c + 1) * P], w20[:, g, c, :],
                                      start=(c == 0), stop=(c == 1))
                        last.then_inc(out_mm, 1)

            def split_mm(dst, sH, sL, mH, mL, start, stop):
                mm(dst, sH, mH, start=start, stop=False)
                mm(dst, sH, mL, start=False, stop=False)
                return mm(dst, sL, mH, start=False, stop=stop)

            def a_tile(graph, acc, which, H, L, j, last_stop):
                if j % HB == 0:
                    pe.wait_ge(vH[which], cnt(graph, 2, j // HB + 1))
                    pe.wait_ge(vL[which], cnt(graph, 2, j // HB + 1))
                for g in range(2):
                    last = split_mm(acc[g][:, :], blk(H, j), blk(L, j), adjH[:, tile_cols(graph, j, g * HALF, HALF)],
                                    adjL[:, tile_cols(graph, j, g * HALF, HALF)], j == 0, last_stop and j == NB - 1)
                    if last_stop and j == NB - 1 and which == 2:
                        last.then_inc(a2_mm, 1)
                return last

            def phase_p(b, p):
                if b is not None:
                    pe.wait_ge(summed, cnt(b, 2 * (NB - 1), 2 * (NB - 1)))
                    if p is not None:
                        pe.wait_ge(vL[1], cnt(b, 2, 2))
                    for k in range(NB):
                        last = mm(acc3[0][:, k:k + 1], blk(rowsum, k), ones[:, :], start=True, stop=True)
                    last.then_inc(rs_mm, 1)
                for j in range(NB):
                    if b is not None:
                        if p is not None and j == 0:
                            pe.wait_ge(nb_copied, cnt(p, 1, 1))
                            pe.wait_ge(nb_copied2, cnt(p, 1, 1))
                        pe.wait_ge(lo_ready, cnt(b, NB, j + 1))
                        a_tile(b, acc12, 1, v1H, v1L, j, False)
                    if p is not None and j in (1, 2):
                        g = j - 1
                        pe.wait_ge(nb_copied if g == 0 else nb_copied2, cnt(p, 1, 1))
                        for k in range(HB):
                            last = mm(blk(hid[g], k), blk(colT, g * HB + k), wneigh[:, :], start=True, stop=True)
                        last.then_inc(p2_mm, 1)
                if b is not None:
                    for g in range(2):
                        for k in range(HB):
                            n = g * HB + k
                            last = split_mm(blk(acc12[g], k), blk(v1H, n), blk(v1L, n), epsH[:, :], epsL[:, :],
                                            False, k == HB - 1)
                        last.then_inc(a1_mm, 1)

            def phase_q(b, p):
                for s in range(NB + HB - 1):
                    if b is not None and s < NB:
                        if s % HB == 0:
                            pe.wait_ge(agg_copied if s == 0 else agg_copied2, cnt(b, 1, 1))
                        if s >= 2:
                            pe.wait_ge(weighted, cnt(b, NB, s - 1))
                            pe.wait_ge(squared, cnt(b, NB, s - 1))
                        elif p is not None:
                            pe.wait_ge(z_done, cnt(p, 2, s + 1))
                        mm(hid[s % 2][:, :], blk(colT, s), w1[:, :], start=True, stop=False)
                        mm(hid[s % 2][:, :], onesR[:, :], b1R[:, :], start=False, stop=True).then_inc(w1_mm, 1)
                    if p is not None and s < 2:
                        layer3_turn(b, p, s)
                    if p is not None and 1 <= s < 3:
                        layer3_transform(p, s - 1)
                    if p is not None and s >= HB - 1:
                        j = s - (HB - 1)
                        if j == 0:
                            pe.wait_ge(v3_steps, cnt(p, 4, 4))
                        a_tile(p, acc3, 3, v3H, v3L, j, True).then_inc(a3_tile, 1)
                    if b is not None and 1 <= s <= NB:
                        k = s - 1
                        pe.wait_ge(silu_done, cnt(b, NB, k + 1))
                        if k >= 1:
                            pe.wait_ge(sT_copied, cnt(b, NB, k))
                        elif p is not None:
                            pe.wait_ge(p1_copied, cnt(p, 2, 1))
                        for h in range(KH):
                            last = nc.tensor.transpose(blk(turn, h), blk(u, h), ident[:, :])
                        last.then_inc(turn_mm, 1)
                    if b is not None and 2 <= s <= NB + 1:
                        k = s - 2
                        pe.wait_ge(sT_copied, cnt(b, NB, k + 1))
                        if k >= 1:
                            pe.wait_ge(x1_done, cnt(b, NB, k))
                        elif p is not None:
                            pe.wait_ge(p1_copied, cnt(p, 2, 2))
                        for h in range(KH):
                            last = mm(mlp[:, 0:D], blk(sT, h), blk(w2, h), start=(h == 0), stop=(h == KH - 1))
                        last.then_inc(w2_mm, 1)
                    if b is not None and s == NB + 2:
                        xn_turn(b, 0)

            def layer3_turn(b, p, g):
                pe.wait_ge(relu_done["ln3"], cnt(p, 2, g + 1))
                if g == 0:
                    if b is not None:
                        pe.wait_ge(deg_steps, cnt(b, 4, 1))
                    else:
                        pe.wait_ge(o_scaled, cnt(p - 1, 2, 2))
                else:
                    pe.wait_ge(hT_copied, cnt(p, 2, g))
                for k in range(HB):
                    last = nc.tensor.transpose(blk(acc3[0], k), blk(t[g], k), ident[:, :])
                last.then_inc(hT_mm, 1)

            def layer3_transform(p, g):
                pe.wait_ge(hT_copied, cnt(p, 2, g + 1))
                if g == 1:
                    pe.wait_ge(v3_steps, cnt(p, 4, 1))
                for k in range(HB):
                    last = mm(blk(acc3[1], k), blk(fT, k), w3[:, :], start=True, stop=True)
                last.then_inc(t3_mm, 1)

            def xn_turn(b, g):
                pe.wait_ge(xn_steps, cnt(b, 4, 2 * g + 2))
                pe.wait_ge(weighted, cnt(b, NB, NB - 1 + g))
                pe.wait_ge(squared, cnt(b, NB, NB - 1 + g))
                for k in range(HB):
                    last = nc.tensor.transpose(blk(hid[g], k), blk(xn, k), ident[:, :])
                last.then_inc(xnT_mm, 1)

            def xn_self(b, g):
                pe.wait_ge(xnT_copied, cnt(b, 2, g + 1))
                if g == 0:
                    pe.wait_ge(sT_copied, cnt(b, NB, NB))
                else:
                    pe.wait_ge(x1_done, cnt(b, NB, NB))
                for k in range(HB):
                    last = mm(blk(p1_bank[g], k), blk(fT, k), wsum[:, :], start=True, stop=True)
                last.then_inc(p1_mm, 1)

            def phase_r(b, p):
                if b is not None:
                    xn_self(b, 0)
                for j in range(NB):
                    if b is not None:
                        a_tile(b, acc12, 2, v2H, v2L, j, True)
                    if p is not None and j == 1:
                        for g in range(2):
                            pe.wait_ge(o_copied if g == 0 else o_copied2, cnt(p, 1, 1))
                            for k in range(HB):
                                last = nc.tensor.transpose(blk(acc3[g], k), blk(colT, g * HB + k), ident[:, :])
                            last.then_inc(oT_mm, 1)
                    if b is not None and j == HB - 1:
                        xn_turn(b, 1)
                    if b is not None and j == HB:
                        xn_self(b, 1)

            layer0()
            phase_p(0, None)
            phase_q(0, None)
            phase_r(0, None)
            with pe.Fori(1, B) as i:
                phase_p(i, i - 1)
                phase_q(i, i - 1)
                phase_r(i, i - 1)
            phase_p(None, B - 1)
            phase_q(None, B - 1)
            phase_r(None, B - 1)

        @block.scalar
        def _(act):
            a = nc.scalar.activation

            for dst, name in ((xr, "x0"), (mask0, "mask0"), (member, "member0")):
                act.dma_start(dst[:], t_in[name]).then_inc(l0_in, 16)
            act.wait_ge(s0_pool, 1)
            for tt in range(T0):
                for q in range(4):
                    act.dma_start(adj0[q * S0:(q + 1) * S0, tt, q * S0:(q + 1) * S0],
                                  adjT_d[4 * tt + q, 0:S0, 0:S0]).then_inc(l0_in, 16)
            act.dma_start(fus[:, :], t_in["L0_gnn_fusion_w"].partition_broadcast(P)).then_inc(l0_in, 16)
            act.dma_start(ident[:, :], t_in["ident"]).then_inc(l0_in, 16)
            for dst, name in ((w10, "w10"), (w20, "w20")):
                act.dma_start(dst[:], t_in[name]).then_inc(l0_w, 16)
            act.dma_start(b10[:, :], t_in["L0_gnn_b1"].partition_broadcast(P)).then_inc(l0_w, 16)
            act.dma_start(b20[:, :], t_in["L0_gnn_b2"].partition_broadcast(P)).then_inc(l0_w, 16)
            for dst, name in ((w1, "L1_gnn_W1"), (w2, "w2"), (wneigh, "L2_gnn_W_neigh"), (wself, "L2_gnn_W_self"),
                              (w3, "w3T")):
                act.dma_start(dst[:], t_in[name]).then_inc(w_in, 16)
            for dst, name in ((wrms, "L1_gnn_rms_weight"), (b2bc, "L1_gnn_b2"), (gam, "L2_gnn_gamma"),
                              (bet, "L2_gnn_beta"), (b3bc, "L3_gnn_b"), (eps, "L1_gnn_epsilon")):
                act.dma_start(dst[:], t_in[name].partition_broadcast(P)).then_inc(w_in, 16)
            act.dma_start(b1r2[:, :], t_in["L1_gnn_b1"].partition_broadcast(2)).then_inc(w_in, 16)

            def split_hi(c, j):
                act.wait_ge(raw_in[j % RS], cnt(c, 16 * (NB // RS), 16 * (j // RS + 1)))
                if not isinstance(c, int) or c >= 2:
                    act.wait_ge(a3_tile, cnt(c - 2, NB, j + 1))
                if j == 0 and (not isinstance(c, int) or c >= 1):
                    act.wait_ge(deg_steps, cnt(c - 1, 4, 3))
                a(adjH[:, tile_cols(c, j, 0, N)], raw[:, j % RS, :], ACT.Copy,
                  accum_out=deg[:, NB + j:NB + j + 1]).then_inc(hi_ready, 1)

            def layer0():
                act.wait_ge(s0_dve, 5)
                a(fex[:, :], fus[:, :], ACT.Exp, bias=fmx[:, 1:2], accum_out=fsum[:, 0:1]).then_inc(s0_act, 1)
                act.wait_ge(s0_dve, 8)
                a(h0[:].rearrange("p t d -> p (t d)"), h0[:].rearrange("p t d -> p (t d)"), ACT.Relu).then_inc(s0_act, 1)
                act.wait_ge(s0_pe, 2)
                for tt in range(T0):
                    a(gt1[:, tt, 0:HALF], acc3[tt][:, :], ACT.Copy)
                    a(gt1[:, tt, HALF:], hid[tt][:, 0:P], ACT.Copy).then_inc(s0_act, 1)
                for q in range(T0 * G0):
                    act.wait_ge(c1_scaled, q + 1)
                    a(h10[:, q % 2, :], h10[:, q % 2, :], ACT.Relu).then_inc(c1_relu, 1)
                    act.wait_ge(g2_mm, q + 1)
                    need(act, out_mm, q - 1)
                    a(gt2[:, q % 2, :], turn[:, 0:E0], ACT.Copy).then_inc(g2_copied, 1)
                    if q < NB:
                        split_hi(0, q)

            def relu(kind, graph, g):
                act.wait_ge(ln_steps[kind], cnt(graph, 8, 4 * g + 4))
                a(t[g][:, :], t[g][:, :], ACT.Relu).then_inc(relu_done[kind], 1)

            def v_hi(which, H, graph, g, ready, value):
                act.wait_ge(ready, value)
                a(H[:, g * HALF:(g + 1) * HALF], t[g][:, :], ACT.Copy).then_inc(vH[which], 1)

            def phase_p(b, p):
                if p is not None:
                    for g in range(2):
                        act.wait_ge(p1_mm, cnt(p, 2, g + 1))
                        a(z[g][:, :], p1_bank[g][:, :], ACT.Copy).then_inc(p1_copied, 1)
                    for g in range(2):
                        act.wait_ge(xz_done, cnt(p, 2, g + 1))
                        a(z[g][:, :], z[g][:, :], ACT.Abs).then_inc(sp_steps, 1)
                    for g in range(2):
                        act.wait_ge(sp_steps, cnt(p, 6, 1 + g))
                        a(z[g][:, :], z[g][:, :], ACT.Exp, scale=-1.0).then_inc(sp_steps, 1)
                    for g in range(2):
                        act.wait_ge(sp_steps, cnt(p, 6, 3 + g))
                        a(z[g][:, :], z[g][:, :], ACT.Ln, bias=1.0).then_inc(sp_steps, 1)
                    relu("ln3", p, 0)
                if b is not None:
                    act.wait_ge(a1_mm, cnt(b, 2, 1))
                    if p is not None:
                        act.wait_ge(p2_mm, cnt(p, 2, 2))
                    a(colT[:, 0:HALF], acc12[0][:, :], ACT.Copy).then_inc(agg_copied, 1)
                if p is not None:
                    relu("ln3", p, 1)

            def phase_q(b, p, c):
                for s in range(NB + HB - 1):
                    if p is not None and s in (0, 1):
                        if s == 0:
                            turn3_copy(p, 0)
                    if b is not None and s < NB:
                        act.wait_ge(w1_mm, cnt(b, NB, s + 1))
                        if s >= 2:
                            act.wait_ge(msq, cnt(b, NB, s - 1))
                        if not isinstance(b, int) or b or s:
                            act.wait_ge(squared, cnt(b, NB, s))
                        a(junk[:, :], hid[s % 2][:, :], ACT.Square, scale=HID ** -0.5,
                          accum_out=ss[:, s % 2:s % 2 + 1]).then_inc(squared, 1)
                    if p is not None and s == 1:
                        turn3_copy(p, 1)
                    if b is not None and 1 <= s <= NB:
                        k = s - 1
                        act.wait_ge(rms, cnt(b, NB, k + 1))
                        act.wait_ge(weighted, cnt(b, NB, k + 1))
                        a(u[:, :], u[:, :], ACT.Silu, scale=rrms[:, k % 2:k % 2 + 1]).then_inc(silu_done, 1)
                    if p is not None and s in (2, 3):
                        v_hi(3, v3H, p, s - 2, v3_steps, cnt(p, 4, 2 * (s - 2) + 2))
                    if c is not None and s >= HB:
                        split_hi(c, s - HB)
                    if b is not None and 1 <= s <= NB:
                        k = s - 1
                        act.wait_ge(turn_mm, cnt(b, NB, k + 1))
                        if k >= 1:
                            act.wait_ge(w2_mm, cnt(b, NB, k))
                        a(sT[:, :], turn[:, :], ACT.Copy).then_inc(sT_copied, 1)
                    if b is not None and s == 7:
                        relu("ln2a", b, 0)
                if b is not None:
                    v_hi(2, v2H, b, 0, v2_scaled, cnt(b, 2, 1))

            def turn3_copy(p, g):
                act.wait_ge(hT_mm, cnt(p, 2, g + 1))
                if g == 1:
                    act.wait_ge(t3_mm, cnt(p, 2, 1))
                else:
                    act.wait_ge(p1_mm, cnt(p, 2, 2))
                a(fT[:, :], acc3[0][:, :], ACT.Copy).then_inc(hT_copied, 1)

            def phase_r(b, p, c):
                if b is not None:
                    act.wait_ge(xnT_mm, cnt(b, 2, 1))
                    if p is not None:
                        act.wait_ge(t3_mm, cnt(p, 2, 2))
                    a(fT[:, :], hid[0][:, :], ACT.Copy).then_inc(xnT_copied, 1)
                if p is not None:
                    act.wait_ge(a3_tile, cnt(p, NB, NB))
                    if b is not None:
                        act.wait_ge(w1_mm, cnt(b, NB, NB))
                    a(colT[:, 0:HALF], acc3[0][:, :], ACT.Copy).then_inc(o_copied, 1)
                if c is not None:
                    split_hi(c, NB - 1)
                if b is not None:
                    relu("ln2a", b, 1)
                if c is not None:
                    relu("ln1", c, 0)
                    v_hi(1, v1H, c, 0, relu_done["ln1"], cnt(c, 2, 1))
                if b is not None:
                    v_hi(2, v2H, b, 1, v2_scaled, cnt(b, 2, 2))
                    act.wait_ge(xnT_mm, cnt(b, 2, 2))
                    act.wait_ge(p1_mm, cnt(b, 2, 1))
                    a(fT[:, :], hid[1][:, :], ACT.Copy).then_inc(xnT_copied, 1)
                if c is not None:
                    relu("ln1", c, 1)
                    v_hi(1, v1H, c, 1, relu_done["ln1"], cnt(c, 2, 2))
                if b is not None:
                    act.wait_ge(a2_mm, cnt(b, 2, 1))
                    if p is not None:
                        act.wait_ge(oT_mm, cnt(p, 2, 2))
                    a(colT[:, 0:HALF], acc12[0][:, :], ACT.Copy).then_inc(nb_copied, 1)

            layer0()
            for g in range(2):
                relu("ln1", 0, g)
                v_hi(1, v1H, 0, g, relu_done["ln1"], cnt(0, 2, g + 1))
            phase_p(0, None)
            phase_q(0, None, 1)
            phase_r(0, None, 1)
            with act.Fori(1, B - 1) as i:
                phase_p(i, i - 1)
                phase_q(i, i - 1, i + 1)
                phase_r(i, i - 1, i + 1)
            phase_p(B - 1, B - 2)
            phase_q(B - 1, B - 2, None)
            phase_r(B - 1, B - 2, None)
            phase_p(None, B - 1)
            phase_q(None, B - 1, None)
            phase_r(None, B - 1, None)

        @block.vector
        def _(dve):
            v = nc.vector

            def setup():
                v.memset(ones[:, :], 1.0)
                v.memset(rms_eps[:, :], 1e-6)
                v.memset(power[:, :], -0.5).then_inc(const_ready, 1)

            def layer0():
                dve.wait_ge(l0_in, 16 * 13)
                i2 = ident[:, :].unsqueeze(1).broadcast_to([P, T0, P])
                v.tensor_tensor(adj0[:], adj0[:], i2, ALU.add).then_inc(s0_dve, 1)
                dve.wait_ge(s0_dve, 1)
                for tt in range(T0):
                    last = v.tensor_tensor(ma[:, tt, :, :], mask0[:], adj0[:, tt, :].unsqueeze(1)
                                           .broadcast_to([P, G0, P]), ALU.mult)
                last.then_inc(s0_dve, 1)
                v.tensor_reduce(fmx[:, 0:1], fus[:, :], AX.X, ALU.max).then_inc(s0_dve, 1)
                for tt in range(T0):
                    last = v.bn_stats(st0[:, tt, :], xr[:, tt, :])
                last.then_inc(s0_dve, 1)
                dve.wait_ge(s0_dve, 4)
                for tt in range(T0):
                    v.bn_aggr(mv0[:, tt, :], st0[:, tt, :])
                v.tensor_scalar(fmx[:, 1:2], fmx[:, 0:1], -1.0, None, ALU.mult).then_inc(s0_dve, 1)
                dve.wait_ge(s0_dve, 5)
                v.tensor_scalar(ve0[:, :], mv0[:, :, 1], 1e-5, None, ALU.add).then_inc(s0_dve, 1)
                dve.wait_ge(s0_pe, 1)
                v.tensor_scalar(dg0[:, 0, :], acc12[0][:, 0:T0 * G0], 0.0, None, ALU.is_equal)
                v.tensor_scalar(dg0[:, 1, :], acc12[0][:, 0:T0 * G0], 0.0, None, ALU.not_equal).then_inc(s0_own, 1)
                dve.wait_ge(s0_own, 1)
                v.tensor_tensor(dg0[:, 2, :], acc12[0][:, 0:T0 * G0], dg0[:, 0, :], ALU.add).then_inc(s0_dve, 1)
                dve.wait_ge(s0_pool, 2)
                for tt in range(T0):
                    last = v.tensor_scalar(h0[:, tt, :], xr[:, tt, :], mv0[:, tt, 0:1], rs0[:, tt:tt + 1],
                                           ALU.subtract, ALU.mult)
                last.then_inc(s0_dve, 1)
                dve.wait_ge(s0_pool, 3)
                v.tensor_tensor(di0[:, :], dg0[:, 3, :], dg0[:, 1, :], ALU.mult).then_inc(s0_own, 1)
                dve.wait_ge(s0_own, 2)
                for q in range(T0 * G0):
                    m = ma[:, q // G0, q % G0, :]
                    last = v.tensor_scalar(m, m, di0[:, q:q + 1], None, ALU.mult)
                last.then_inc(s0_dve, 1)
                dve.wait_ge(s0_act, 1)
                v.reciprocal(fsum[:, 1:2], fsum[:, 0:1]).then_inc(s0_own, 1)
                dve.wait_ge(s0_own, 3)
                v.scalar_tensor_tensor(cw[:, :], fex[:, :], fsum[:, 1:2], member[:, :], ALU.mult, ALU.mult
                                       ).then_inc(s0_dve, 1)
                dve.wait_ge(s0_dve, 10)
                dve.wait_ge(l0_w, 16 * 4)
                Q0 = T0 * G0
                for q in range(Q0 + 2):
                    if q < Q0:
                        g = q % G0
                        dve.wait_ge(c1_mm, q + 1)
                        need(dve, g2_mm, q - 1)
                        v.scalar_tensor_tensor(h10[:, q % 2, :], hid[q % 2][:, 0:E0], di0[:, q:q + 1],
                                               b10[:, g * E0:(g + 1) * E0], ALU.mult, ALU.add
                                               ).then_inc(c1_scaled, 1)
                    if q >= 2:
                        r = q - 2
                        tt, g = r // G0, r % G0
                        dve.wait_ge(out_mm, r + 1)
                        v.scalar_tensor_tensor(o0[:, 0, :], mlp[:, 0:D], di0[:, r:r + 1],
                                               b20[:, g * D:(g + 1) * D], ALU.mult, ALU.add).then_inc(out_scaled, 1)
                        dve.wait_ge(out_scaled, r + 1)
                        v.tensor_scalar(o0[:, 1, :], o0[:, 0, :], 0.0, cw[:, g:g + 1], ALU.max, ALU.mult
                                        ).then_inc(out_weighted, 1)
                        dve.wait_ge(out_weighted, r + 1)
                        v.tensor_tensor(xr[:, tt, :], xr[:, tt, :], o0[:, 1, :], ALU.add).then_inc(x0_added, 1)
                        dve.wait_ge(x0_added, r + 1)
                    if 1 <= q <= NB:
                        split_lo(0, q - 1)

            def weights():
                dve.wait_ge(w_in, 16 * 12)
                v.tensor_tensor(wsum[:, :], wself[:, :], wneigh[:, :], ALU.add)
                v.tensor_scalar(epsI[:, :], ident[:, :], eps[:, 0:1], None, ALU.mult)
                v.tensor_copy(b1hi[:, :], b1r2[:, :])
                v.tensor_copy(onesR[:, :], ones[0:2, :].broadcast_to([2, P])).then_inc(const_ready, 1)
                dve.wait_ge(const_ready, 2)
                v.tensor_copy(epsH[:, :], epsI[:, :])
                v.tensor_tensor(b1lo[:, :], b1r2[:, :], b1hi[:, :].bitcast(F32), ALU.subtract).then_inc(const_ready, 1)
                dve.wait_ge(const_ready, 3)
                v.tensor_tensor(epsL[:, :], epsI[:, :], epsH[:, :].bitcast(F32), ALU.subtract)
                v.tensor_scalar(b1lo[:, :], b1lo[:, :], ident[0:2, 1:2], None, ALU.mult).then_inc(const_ready, 1)
                dve.wait_ge(const_ready, 4)
                v.scalar_tensor_tensor(b1R[:, :], b1hi[:, :].bitcast(F32), ident[0:2, 0:1], b1lo[:, :],
                                       ALU.mult, ALU.add).then_inc(const_ready, 1)

            def split_lo(c, j):
                dve.wait_ge(hi_ready, cnt(c, NB, j + 1))
                cols = tile_cols(c, j, 0, N)
                v.tensor_tensor(adjL[:, cols], raw[:, j % RS, :], adjH[:, cols].bitcast(F32), ALU.subtract
                                ).then_inc(lo_ready, 1)

            def norm(kind, graph, g, source):
                steps = ln_steps[kind]
                v.tensor_copy(tick[:, 0:1], power[:, 0:1])
                for k in range(HB):
                    last = v.bn_stats(stat6[:, k, :], source(k))
                last.then_inc(steps, 1)
                dve.wait_ge(steps, cnt(graph, 8, 4 * g + 1))
                v.tensor_copy(tick[:, 1:2], power[:, 0:1])
                for k in range(HB):
                    last = v.bn_aggr(mv[g][:, k, :], stat6[:, k, :])
                last.then_inc(steps, 1)
                dve.wait_ge(steps, cnt(graph, 8, 4 * g + 2))
                v.tensor_scalar(veps[g][:, :], mv[g][:, :, 1], 1e-5, None, ALU.add).then_inc(steps, 1)

            def norm_scale(kind, graph, g, source):
                dve.wait_ge(ln_rstd[kind], cnt(graph, 2, g + 1))
                for k in range(HB):
                    last = v.tensor_scalar(blk(t[g], k), source(k), mv[g][:, k, 0:1], rstd[g][:, k:k + 1],
                                           ALU.subtract, ALU.mult)
                last.then_inc(ln_steps[kind], 1)

            def v_lo(which, H, L, graph, g):
                dve.wait_ge(vH[which], cnt(graph, 2, g + 1))
                cols = slice(g * HALF, (g + 1) * HALF)
                v.tensor_tensor(L[:, cols], t[g][:, :], H[:, cols].bitcast(F32), ALU.subtract).then_inc(vL[which], 1)

            def xsrc(graph, g):
                return lambda k: xcols(graph, g * HB + k, 1)

            def tsrc(g):
                return lambda k: blk(t[g], k)

            def degrees(b, p):
                if p is not None:
                    v.tensor_copy(sc_p[:, :], sc_b[:, :])
                dve.wait_ge(rs_mm, cnt(b, 1, 1))
                v.tensor_copy(deg[:, 0:NB], acc3[0][:, 0:NB]).then_inc(deg_steps, 1)
                dve.wait_ge(deg_steps, cnt(b, 4, 1))
                dve.wait_ge(hi_ready, cnt(b, NB, NB))
                v.tensor_scalar(dz[:, :], deg[:, :], 0.0, None, ALU.is_equal)
                v.tensor_scalar(dnz[:, 0:NB], deg[:, 0:NB], 0.0, None, ALU.not_equal)
                v.tensor_scalar(dnz[:, NB:], deg[:, NB:], 0.0, -1.0, ALU.not_equal, ALU.mult).then_inc(deg_steps, 1)
                dve.wait_ge(deg_steps, cnt(b, 4, 2))
                v.tensor_tensor(dsafe[:, :], deg[:, :], dz[:, :], ALU.add).then_inc(deg_steps, 1)

            def degrees_end(b):
                dve.wait_ge(deg_pow, cnt(b, 1, 1))
                v.tensor_tensor(sc_b[:, :], dpow[:, :], dnz[:, :], ALU.mult).then_inc(deg_steps, 1)

            def phase_p(b, p):
                if b is not None:
                    degrees(b, p)
                elif p is not None:
                    v.tensor_copy(sc_p[:, :], sc_b[:, :]).then_inc(sc_p_last, 1)
                    dve.wait_ge(sc_p_last, 1)
                if p is not None:
                    if b is not None:
                        dve.wait_ge(deg_steps, cnt(b, 4, 2))
                    for g in range(2):
                        dve.wait_ge(p1_copied, cnt(p, 2, g + 1))
                        dve.wait_ge(p2_mm, cnt(p, 2, g + 1))
                        for k in range(HB):
                            n = g * HB + k
                            last = v.scalar_tensor_tensor(blk(z[g], k), blk(hid[g], k), sc_p[:, NB + n:NB + n + 1],
                                                          blk(z[g], k), ALU.mult, ALU.add)
                        last.then_inc(z_done, 1)
                        dve.wait_ge(z_done, cnt(p, 2, g + 1))
                        v.scalar_tensor_tensor(xcols(p, g * HB, HB), z[g][:, :], 0.0, xcols(p, g * HB, HB),
                                               ALU.max, ALU.add).then_inc(xz_done, 1)
                if b is not None:
                    degrees_end(b)
                if p is not None:
                    for g in range(2):
                        dve.wait_ge(sp_steps, cnt(p, 6, 5 + g))
                        v.tensor_tensor(xcols(p, g * HB, HB), xcols(p, g * HB, HB), z[g][:, :], ALU.add
                                        ).then_inc(x2_done, 1)
                        dve.wait_ge(x2_done, cnt(p, 2, g + 1))
                        norm("ln3", p, g, xsrc(p, g))
                        norm_scale("ln3", p, g, xsrc(p, g))
                if b is not None:
                    dve.wait_ge(a1_mm, cnt(b, 2, 2))
                    if p is not None:
                        dve.wait_ge(p2_mm, cnt(p, 2, 2))
                    v.tensor_copy(colT[:, HALF:], acc12[1][:, :]).then_inc(agg_copied2, 1)

            def phase_q(b, p, c):
                for s in range(NB + HB - 1):
                    if b is not None and s < NB:
                        dve.wait_ge(w1_mm, cnt(b, NB, s + 1))
                        if s >= 1:
                            dve.wait_ge(turn_mm, cnt(b, NB, s))
                        dve.wait_ge(squared, cnt(b, NB, s + 1))
                        v.tensor_tensor(u[:, :], hid[s % 2][:, :], wrms[:, :], ALU.mult).then_inc(weighted, 1)
                    if p is not None and s in (1, 2):
                        g = s - 1
                        dve.wait_ge(t3_mm, cnt(p, 2, g + 1))
                        v.tensor_tensor(by_block(t[g][:, :]), by_block(acc3[1][:, :]), over_blocks(b3bc), ALU.add
                                        ).then_inc(v3_steps, 1)
                        dve.wait_ge(v3_steps, cnt(p, 4, 2 * g + 1))
                        for k in range(HB):
                            n = g * HB + k
                            last = v.tensor_scalar(blk(t[g], k), blk(t[g], k), sc_p[:, n:n + 1], None, ALU.mult)
                        last.then_inc(v3_steps, 1)
                    if p is not None and s in (2, 3):
                        v_lo(3, v3H, v3L, p, s - 2)
                    if b is not None and 2 <= s <= NB + 1:
                        k = s - 2
                        dve.wait_ge(w2_mm, cnt(b, NB, k + 1))
                        if k == 0:
                            dve.wait_ge(xb2, cnt(b, 1, 1))
                        v.tensor_tensor(xcols(b, k, 1), xcols(b, k, 1), mlp[:, 0:D], ALU.add).then_inc(x1_done, 1)
                    if c is not None and s >= HB:
                        split_lo(c, s - HB)
                    if b is not None and s == 6:
                        dve.wait_ge(x1_done, cnt(b, NB, HB))
                        norm("ln2a", b, 0, xsrc(b, 0))
                        norm_scale("ln2a", b, 0, xsrc(b, 0))
                    if b is not None and s == 8:
                        xn_norm(b, 0)
                    if b is not None and s == 10:
                        xn_scale(b, 0)

            def xn_norm(b, g):
                dve.wait_ge(relu_done["ln2a"], cnt(b, 2, g + 1))
                norm("ln2b", b, g, tsrc(g))
                norm_scale("ln2b", b, g, tsrc(g))

            def xn_scale(b, g):
                dve.wait_ge(xn_steps, cnt(b, 4, 2 * g + 2))
                for k in range(HB):
                    n = g * HB + k
                    last = v.tensor_scalar(blk(t[g], k), blk(xn, k), sc_b[:, n:n + 1], None, ALU.mult)
                last.then_inc(v2_scaled, 1)

            def phase_r(b, p, c):
                if p is not None:
                    dve.wait_ge(a3_tile, cnt(p, NB, NB))
                    if b is not None:
                        dve.wait_ge(w1_mm, cnt(b, NB, NB))
                    v.tensor_copy(colT[:, HALF:], acc3[1][:, :]).then_inc(o_copied2, 1)
                if b is not None:
                    v_lo(2, v2H, v2L, b, 0)
                if b is not None:
                    dve.wait_ge(x1_done, cnt(b, NB, NB))
                    norm("ln2a", b, 1, xsrc(b, 1))
                    norm_scale("ln2a", b, 1, xsrc(b, 1))
                if c is not None:
                    ln1(c, 0)
                if b is not None:
                    xn_norm(b, 1)
                if c is not None:
                    v_lo(1, v1H, v1L, c, 0)
                    split_lo(c, NB - 1)
                if p is not None:
                    for g in range(2):
                        dve.wait_ge(oT_mm, cnt(p, 2, g + 1))
                        if b is not None and g == 0:
                            dve.wait_ge(w2_mm, cnt(b, NB, NB))
                        if b is not None and g == 1:
                            dve.wait_ge(turn_mm, cnt(b, NB, NB))
                        s_in = sc_p[:, g * HB:(g + 1) * HB].unsqueeze(2).broadcast_to([P, HB, D])
                        v.scalar_tensor_tensor(by_block(z[g][:, :]), by_block(acc3[g][:, :]), 0.0, s_in,
                                               ALU.max, ALU.mult).then_inc(o_scaled, 1)
                        dve.wait_ge(o_scaled, cnt(p, 2, g + 1))
                        v.tensor_tensor(xcols(p, g * HB, HB), xcols(p, g * HB, HB), z[g][:, :], ALU.add
                                        ).then_inc(x3_done, 1)
                        if b is not None and g == 0:
                            xn_scale(b, 1)
                elif b is not None:
                    xn_scale(b, 1)
                if b is not None:
                    v_lo(2, v2H, v2L, b, 1)
                if c is not None:
                    ln1(c, 1)
                    v_lo(1, v1H, v1L, c, 1)
                if b is not None:
                    dve.wait_ge(a2_mm, cnt(b, 2, 2))
                    if p is not None:
                        dve.wait_ge(oT_mm, cnt(p, 2, 2))
                    v.tensor_copy(colT[:, HALF:], acc12[1][:, :]).then_inc(nb_copied2, 1)

            def ln1(c, g):
                if g == 0:
                    dve.wait_ge(x0_in, cnt(c, 16, 16))
                norm("ln1", c, g, xsrc(c, g))
                norm_scale("ln1", c, g, xsrc(c, g))

            setup()
            layer0()
            weights()
            for g in range(2):
                ln1(0, g)
            for g in range(2):
                v_lo(1, v1H, v1L, 0, g)
            phase_p(0, None)
            phase_q(0, None, 1)
            phase_r(0, None, 1)
            with dve.Fori(1, B - 1) as i:
                phase_p(i, i - 1)
                phase_q(i, i - 1, i + 1)
                phase_r(i, i - 1, i + 1)
            phase_p(B - 1, B - 2)
            phase_q(B - 1, B - 2, None)
            phase_r(B - 1, B - 2, None)
            phase_p(None, B - 1)
            phase_q(None, B - 1, None)
            phase_r(None, B - 1, None)

        @block.gpsimd
        def _(pool):
            gp = nc.gpsimd

            def pw(dst, src, n):
                return gp.tensor_tensor(dst, src, power[:, 0:n], ALU.pow)

            def add_rows(c, j):
                pool.wait_ge(raw_in[j % RS], cnt(c, 16 * (NB // RS), 16 * (j // RS + 1)))
                n = 2 * (NB - 1)
                for h in range(2):
                    cols = slice(h * HALF, (h + 1) * HALF)
                    if j == 1:
                        if h == 0:
                            pool.wait_ge(raw_in[0], cnt(c, 16 * (NB // RS), 16))
                            if not isinstance(c, int) or c >= 1:
                                pool.wait_ge(rs_mm, cnt(c - 1, 1, 1))
                        first = raw[:, 0, cols]
                    else:
                        pool.wait_ge(summed, cnt(c, n, 2 * (j - 2) + h + 1))
                        first = rowsum[:, cols]
                    if h == 1:
                        pool.wait_ge(lo_ready, cnt(c, NB, j + 1))
                    gp.tensor_tensor(rowsum[:, cols], first, raw[:, j % RS, cols], ALU.add).then_inc(summed, 1)

            def rstd_of(kind, graph, g):
                pool.wait_ge(ln_steps[kind], cnt(graph, 8, 4 * g + 3))
                pw(rstd[g][:, :], veps[g][:, :], HB).then_inc(ln_rstd[kind], 1)

            def affine(b, g):
                pool.wait_ge(ln_steps["ln2b"], cnt(b, 8, 4 * g + 4))
                if g == 1:
                    pool.wait_ge(xnT_mm, cnt(b, 2, 1))
                    pool.wait_ge(v2_scaled, cnt(b, 2, 1))
                gp.tensor_tensor(by_block(xn[:, :]), by_block(t[g][:, :]), over_blocks(gam), ALU.mult).then_inc(xn_steps, 1)
                pool.wait_ge(xn_steps, cnt(b, 4, 2 * g + 1))
                gp.tensor_tensor(by_block(xn[:, :]), by_block(xn[:, :]), over_blocks(bet), ALU.add).then_inc(xn_steps, 1)

            def phase_p(b, p):
                if b is not None:
                    pool.wait_ge(deg_steps, cnt(b, 4, 3))
                    pw(dpow[:, :], dsafe[:, :], 16).then_inc(deg_pow, 1)
                if p is not None:
                    rstd_of("ln3", p, 0)
                    rstd_of("ln3", p, 1)

            def phase_q(b, p, c):
                for s in range(NB + HB - 1):
                    if b is not None and s < NB:
                        pool.wait_ge(squared, cnt(b, NB, s + 1))
                        if s >= 2:
                            pool.wait_ge(silu_done, cnt(b, NB, s - 1))
                        e = s % 2
                        gp.tensor_tensor(sse[:, e:e + 1], ss[:, e:e + 1], rms_eps[:, :], ALU.add).then_inc(msq, 1)
                        pool.wait_ge(msq, cnt(b, NB, s + 1))
                        pw(rrms[:, e:e + 1], sse[:, e:e + 1], 1).then_inc(rms, 1)
                    if b is not None and s == 6:
                        rstd_of("ln2a", b, 0)
                    if b is not None and s == 8:
                        rstd_of("ln2b", b, 0)
                        affine(b, 0)
                    if c is not None and s >= HB + 1:
                        add_rows(c, s - HB)

            def phase_r(b, p, c):
                if b is not None:
                    rstd_of("ln2a", b, 1)
                if c is not None:
                    rstd_of("ln1", c, 0)
                if b is not None:
                    rstd_of("ln2b", b, 1)
                    affine(b, 1)
                if c is not None:
                    add_rows(c, NB - 1)
                    rstd_of("ln1", c, 1)
                    plus_b2(c)

            def plus_b2(c):
                pool.wait_ge(ln_steps["ln1"], cnt(c, 8, 8))
                gp.tensor_tensor(by_block(xcols(c, 0, NB)), by_block(xcols(c, 0, NB)), over_blocks(b2bc, NB), ALU.add
                                 ).then_inc(xb2, 1)

            gp.memset(adj0[:], 0.0).then_inc(s0_pool, 1)
            pool.wait_ge(const_ready, 1)
            pool.wait_ge(s0_dve, 6)
            pw(rs0[:, :], ve0[:, :], T0).then_inc(s0_pool, 1)
            pool.wait_ge(s0_dve, 7)
            pw(dg0[:, 3, :], dg0[:, 2, :], T0 * G0).then_inc(s0_pool, 1)
            for j in range(1, NB):
                add_rows(0, j)
            pool.wait_ge(x0_added, T0 * G0)
            gp.dma_start(x0_d.rearrange("t p d -> p t d"), xr[:]).then_inc(x0_stored, 16)
            rstd_of("ln1", 0, 0)
            rstd_of("ln1", 0, 1)
            plus_b2(0)
            phase_p(0, None)
            phase_q(0, None, 1)
            phase_r(0, None, 1)
            with pool.Fori(1, B - 1) as i:
                phase_p(i, i - 1)
                phase_q(i, i - 1, i + 1)
                phase_r(i, i - 1, i + 1)
            phase_p(B - 1, B - 2)
            phase_q(B - 1, B - 2, None)
            phase_r(B - 1, B - 2, None)
            phase_p(None, B - 1)


def kernel(**inputs):
    import concourse.bacc as bacc
    from concourse.bass_utils import run_bass_kernel_spmd as run

    def laid(a):
        return np.ascontiguousarray(a)

    x, adj = np.asarray(inputs["x"]), np.asarray(inputs["adj"])
    node = np.arange(P) % S0
    graph = np.arange(P) // S0
    member = np.stack([np.isin(node, g) for g in GROUPS], 1)
    mask = member[:, None, :] & member[None, :, :] & (graph[:, None] == graph[None, :])[:, :, None]
    arrays = {
        "x": x,
        "adjT": adj.transpose(0, 2, 1),
        "x0": x[:, 0:S0].reshape(T0, P, D).transpose(1, 0, 2),
        "mask0": mask.transpose(0, 2, 1).astype(np.float32),
        "member0": member.astype(np.float32),
        "ident": np.eye(P, dtype=np.float32),
        "w10": np.asarray(inputs["L0_gnn_W1"]).transpose(1, 0, 2),
        "w20": np.asarray(inputs["L0_gnn_W2"]).reshape(G0, 2, P, D).transpose(2, 0, 1, 3),
        "L0_gnn_b1": np.asarray(inputs["L0_gnn_b1"]).reshape(-1),
        "L0_gnn_b2": np.asarray(inputs["L0_gnn_b2"]).reshape(-1),
        "w2": np.asarray(inputs["L1_gnn_W2"]).reshape(KH, P, D).transpose(1, 0, 2).reshape(P, KH * D),
        "w3T": np.asarray(inputs["L3_gnn_W"]).T,
        "L1_gnn_epsilon": np.asarray(inputs["L1_gnn_epsilon"]).reshape(1),
    }
    for name in ("L0_gnn_fusion_w", "L1_gnn_W1", "L1_gnn_b1", "L1_gnn_rms_weight", "L1_gnn_b2", "L2_gnn_gamma",
                 "L2_gnn_beta", "L2_gnn_W_self", "L2_gnn_W_neigh", "L3_gnn_b"):
        arrays[name] = np.asarray(inputs[name])
    nc = bacc.Bacc("TRN2", target_bir_lowering=False, num_devices=1)
    arrays = {f"in_{k}": laid(a) for k, a in arrays.items()}
    t_in = {k[3:]: nc.dram_tensor(k, a.shape, F32, kind="ExternalInput").ap() for k, a in arrays.items()}
    out = nc.dram_tensor("out", x.shape, F32, kind="ExternalOutput").ap()
    build(nc, t_in, out)
    return run(nc, [arrays], core_ids=[0]).results[0]["out"]
```

```python
from contextlib import ExitStack

import numpy as np

import concourse.bass as bass
from concourse import mybir

B, N, D, HID = 8, 1024, 128, 512
P = 128
NB = N // P
HB = NB // 2
HALF = N // 2
KH = HID // P
G0, T0, S0 = 5, 2, 32
E0 = 256
N0 = 25
XS = 3
RS = 4
GROUPS = [list(range(25)), [0, 1, 2, 3, 4, 5, 6, 7, 8], [0, 9, 10, 11, 12, 13, 14], [6, 7, 8, 12, 13, 14],
          [3, 4, 5, 9, 10, 11]]

F32 = mybir.dt.float32
F32R = mybir.dt.float32r
ALU = mybir.AluOpType
ACT = mybir.ActivationFunctionType
AX = mybir.AxisListType


def cnt(graph, per_graph, c):
    return graph * per_graph + c


def need(eng, sem, value):
    if isinstance(value, int) and value <= 0:
        return
    eng.wait_ge(sem, value)


def build(nc, t_in, out):
    x_d, adjT_d = t_in["x"], t_in["adjT"]
    x0_d = nc.dram_tensor("x_layer0", (T0, P, D), F32).ap()

    with ExitStack() as ctx:
        def sb(name, shape, dt=F32, where=ctx):
            return where.enter_context(nc.sbuf_tensor(name, shape, dt))

        def sem(name):
            return ctx.enter_context(nc.semaphore(name))

        def bank(name):
            return ctx.enter_context(nc.psum_tensor(name, [P, HALF], F32))

        acc12 = [bank("acc12_0"), bank("acc12_1")]
        acc3 = [bank("acc3_0"), bank("acc3_1")]
        hid = [bank("hid_0"), bank("hid_1")]
        turn = bank("turn")
        mlp = bank("mlp")
        p1_bank = [turn, mlp]

        X = sb("X", [P, XS * N])
        raw = sb("raw", [P, RS, N])
        rowsum = sb("rowsum", [P, N])
        v1H, v1L = sb("v1H", [P, N], F32R), sb("v1L", [P, N], F32R)
        v2H, v2L = sb("v2H", [P, N], F32R), sb("v2L", [P, N], F32R)
        v3H, v3L = sb("v3H", [P, N], F32R), sb("v3L", [P, N], F32R)
        colT = sb("colT", [P, N])
        xn = sb("xn", [P, HALF])
        fT = sb("fT", [P, HALF])
        t = [sb("t_0", [P, HALF]), sb("t_1", [P, HALF])]
        t1 = [sb("t1_0", [P, HALF]), sb("t1_1", [P, HALF])]
        u = [sb("u_0", [P, HALF]), sb("u_1", [P, HALF])]
        sT = sb("sT", [P, HALF])
        z = u
        w1 = sb("w1", [P, HID])
        w2 = sb("w2", [P, HID])
        wneigh = sb("wneigh", [P, D])
        wsum = sb("wsum", [P, D])
        w3 = sb("w3", [P, D])
        ident = sb("ident", [P, P])
        epsH, epsL = sb("epsH", [P, P], F32R), sb("epsL", [P, P], F32R)
        wrms = sb("wrms", [P, HID])
        b2bc, gam, bet, b3bc = sb("b2bc", [P, D]), sb("gam", [P, D]), sb("bet", [P, D]), sb("b3bc", [P, D])
        b1R = sb("b1R", [2, HID], F32R)
        onesR = sb("onesR", [2, P], F32R)
        ones = sb("ones", [P, 1])
        eps = sb("eps", [P, 1])
        power = sb("power", [P, 16])
        stat6 = sb("stat6", [P, HB, 6])
        ln = ["ln1", "ln2a", "ln2b", "ln3"]

        def small(name, *shape):
            return {k: [sb(f"{name}_{k}_{g}", [P, *shape]) for g in range(2)] for k in ln}
        mv, negmean, veps = small("mv", HB, 2), small("negmean", HB), small("veps", HB)
        rstd, shift = small("rstd", HB), small("shift", HB)
        tick = sb("tick", [P, 2])
        junk = sb("junk", [P, HID], mybir.dt.bfloat16)
        ss = sb("ss", [P, 2])
        rms_eps = sb("rms_eps", [P, 1])
        sse = sb("sse", [P, 2])
        rrms = sb("rrms", [P, 2])
        deg = sb("deg", [P, 16])
        dnz = sb("dnz", [P, 16])
        dz = sb("dz", [P, 16])
        dsafe = sb("dsafe", [P, 16])
        dpow = sb("dpow", [P, 16])
        sc_b = sb("sc_b", [P, 16])
        sc_p = sb("sc_p", [P, 16])

        def sb0(name, shape, dt=F32):
            return sb(name, shape, dt, early)
        with ExitStack() as early:
            xr = sb0("xr", [P, T0, D])
            h0 = sb0("h0", [P, T0, D])
            adj0 = sb0("adj0", [P, T0, P])
            member = sb0("member", [P, G0])
            ma = sb0("ma", [P, T0, G0, P])
            gt1 = sb0("gt1", [P, T0, G0 * P])
            mask0 = sb0("mask0", [P, G0, P])
        adjH = sb("adjH", [P, 2 * NB * N], F32R)
        with ExitStack() as early:
            w10 = sb0("w10", [P, G0, E0])
            w20 = sb0("w20", [P, G0, 2, D])
            b10 = sb0("b10", [P, G0 * E0])
            b20 = sb0("b20", [P, G0 * D])
            h10 = sb0("h10", [P, 2, E0])
            gt2 = sb0("gt2", [P, 2, E0])
            o0 = sb0("o0", [P, 2, D])
            fus = sb0("fus", [P, G0])
            fmx = sb0("fmx", [P, 2])
            fex = sb0("fex", [P, G0])
            fsum = sb0("fsum", [P, 2])
            cw = sb0("cw", [P, G0])
            st0 = sb0("st0", [P, T0, 6])
            mv0 = sb0("mv0", [P, T0, 2])
            ve0 = sb0("ve0", [P, T0])
            rs0 = sb0("rs0", [P, T0])
            dg0 = sb0("dg0", [P, 4, T0 * G0])
            di0 = sb0("di0", [P, T0 * G0])
            wself = sb0("wself", [P, D])
            epsI = sb0("epsI", [P, P])
            b1r2 = sb0("b1r2", [2, HID])
            b1hi = sb0("b1hi", [2, HID], F32R)
            b1lo = sb0("b1lo", [2, HID])
        adjL = sb("adjL", [P, 2 * NB * N], F32R)

        l0_in, l0_w, w_in, const_ready = sem("l0_in"), sem("l0_w"), sem("w_in"), sem("const_ready")
        s0_dve, s0_pool, s0_act = sem("layer0_dve"), sem("layer0_pool"), sem("layer0_act")
        s0_own = sem("layer0_dve_own")
        s0_pe, x0_stored = sem("layer0_pe"), sem("x0_stored")
        c1_mm, g2_mm, out_mm = sem("c1_mm"), sem("g2_mm"), sem("out_mm")
        c1_scaled, c1_relu, g2_copied = sem("c1_scaled"), sem("c1_relu"), sem("g2_copied")
        out_scaled, out_weighted, x0_added = sem("out_scaled"), sem("out_weighted"), sem("x0_added")
        raw_in = [sem(f"raw_in_{s}") for s in range(RS)]
        xm_in, x0_in = sem("x_in"), sem("x_layer0_in")
        hi_ready, lo_ready = sem("hi_ready"), sem("lo_ready")
        summed = sem("summed")
        sc_kept = sem("scales_kept")
        rs_mm, deg_steps, deg_pow = sem("rs_mm"), sem("deg_steps"), sem("deg_pow")
        ln_steps = {k: sem(k + "_steps") for k in ln}
        pow_done = {k: sem(k + "_pow") for k in ln}
        ln_rstd = {k: sem(k + "_rstd") for k in ln}
        relu_done = {k: sem(k + "_relu") for k in ("ln1", "ln2a", "ln3")}
        vH = {k: sem(f"v{k}_hi") for k in (1, 2, 3)}
        vL = {k: sem(f"v{k}_lo") for k in (1, 2, 3)}
        xb2 = sem("x_plus_b2")
        a1_mm, a2_mm = sem("a1_mm"), sem("a2_mm")
        a3_tile = sem("a3_tile")
        agg_copied, nb_copied, o_copied = sem("agg_copied"), sem("nb_copied"), sem("o_copied")
        agg_copied2, nb_copied2, o_copied2 = sem("agg_copied2"), sem("nb_copied2"), sem("o_copied2")
        w1_mm, turn_mm, w2_mm = sem("w1_mm"), sem("turn_mm"), sem("w2_mm")
        squared, msq, rms, weighted = sem("squared"), sem("mean_square"), sem("rms"), sem("weighted")
        silu_done, sT_copied, x1_done = sem("silu_done"), sem("sT_copied"), sem("x1_done")
        xn_steps, v2_scaled = sem("xn_steps"), sem("v2_scaled")
        xnT_mm, xnT_copied, p1_mm, p1_copied, p2_mm = (sem(s) for s in ("xnT_mm", "xnT_copied", "p1_mm", "p1_copied", "p2_mm"))
        z_done, xz_done, sp_steps, x2_done = sem("z_done"), sem("x_relu_z"), sem("softplus_steps"), sem("x2_done")
        hT_mm, hT_copied, t3_mm, v3_steps = sem("hT_mm"), sem("hT_copied"), sem("t3_mm"), sem("v3_steps")
        oT_mm, o_scaled, x3_done = sem("oT_mm"), sem("o_scaled"), sem("x3_done")
        stored = [sem("stored_0"), sem("stored_1")]

        def xcols(graph, k0, k):
            return X[:, bass.ds((graph % XS) * N + k0 * D, k * D)]

        def tile_cols(graph, j, c0, c):
            return bass.ds(((graph + 1) % 2) * (NB * N) + j * N + c0, c)

        def blk(ap, k):
            return ap[:, k * D:(k + 1) * D]

        def by_block(ap):
            return ap.rearrange("p (k d) -> p k d", d=D)

        def over_blocks(ap, k=HB):
            return ap[:, :].unsqueeze(1).broadcast_to([P, k, D])

        block = ctx.enter_context(nc.Block())

        @block.sync
        def _(sp):
            def load(c):
                for g in range(2):
                    need(sp, stored[g], cnt(c - XS, 16, 16) if not isinstance(c, int) or c >= XS else 0)
                if isinstance(c, int) and c == 0:
                    load_x(c)
                    load_tiles(c)
                    sp.wait_ge(x0_added, T0 * G0)
                    sp.dma_start(x0_d.rearrange("t p d -> p t d"), xr[:]).then_inc(x0_stored, 16)
                    sp.wait_ge(x0_stored, 16)
                    load_x0(c)
                else:
                    sp.wait_ge(x0_in, cnt(c - 1, 16, 16))
                    load_x(c)
                    load_x0(c)
                    load_tiles(c)

            def load_x(c):
                sp.dma_start(by_block(xcols(c, 0, NB)),
                             x_d[bass.ds(c, 1)].rearrange("a (k p) d -> p (a k) d", p=P)).then_inc(xm_in, 16)

            def load_x0(c):
                sp.wait_ge(xm_in, cnt(c, 16, 16))
                sp.dma_start(xcols(c, 0, 1)[0:N0, :],
                             x0_d.rearrange("t (b n) d -> (t b) n d", n=S0)[bass.ds(c, 1), 0:N0, :]
                             .rearrange("a n d -> (a n) d")).then_inc(x0_in, 16)

            def load_tiles(c):
                for j in range(NB):
                    if j >= RS:
                        sp.wait_ge(lo_ready, cnt(c, NB, (j - RS) // 2 * 2 + 2))
                    elif j == 0 and (not isinstance(c, int) or c):
                        sp.wait_ge(lo_ready, cnt(c - 1, NB, NB))
                        sp.wait_ge(rs_mm, cnt(c - 1, 1, 1))
                    sp.dma_start(raw[:, j % RS, :],
                                 adjT_d[bass.ds(c, 1), j * P:(j + 1) * P, :].rearrange("a p n -> p (a n)")
                                 ).then_inc(raw_in[j % RS], 16)

            def store(p):
                for g in range(2):
                    sp.wait_ge(x3_done, cnt(p, 2, g + 1))
                    sp.dma_start(out[bass.ds(p, 1), g * HALF:(g + 1) * HALF, :].rearrange("a (k p) d -> p (a k) d", p=P),
                                 by_block(xcols(p, g * HB, HB))).then_inc(stored[g], 16)

            load(0)
            load(1)
            load(2)
            store(0)
            with sp.Fori(2, B - 1) as i:
                load(i + 1)
                store(i - 1)
            for p in range(B - 2, B):
                store(p)
            for g in range(2):
                sp.wait_ge(stored[g], 16 * B)

        @block.tensor
        def _(pe):
            mm = nc.tensor.matmul

            def layer0():
                pe.wait_ge(const_ready, 1)
                pe.wait_ge(s0_dve, 2)
                for tt in range(T0):
                    for g in range(G0):
                        last = mm(acc12[0][:, tt * G0 + g:tt * G0 + g + 1], ma[:, tt, g, :], ones[:, :],
                                  start=True, stop=True)
                last.then_inc(s0_pe, 1)
                pe.wait_ge(s0_dve, 9)
                pe.wait_ge(s0_act, 2)
                for tt in range(T0):
                    m = ma[:, tt, :, :].rearrange("p g n -> p (g n)")
                    mm(acc3[tt][:, :], h0[:, tt, :], m[:, 0:HALF], start=True, stop=True)
                    last = mm(hid[tt][:, 0:P], h0[:, tt, :], m[:, HALF:], start=True, stop=True)
                last.then_inc(s0_pe, 1)
                pe.wait_ge(l0_w, 16 * 4)
                pe.wait_ge(s0_act, 4)
                Q0 = T0 * G0
                for q in range(Q0 + 2):
                    if q < Q0:
                        tt, g = q // G0, q % G0
                        need(pe, c1_scaled, q - 1)
                        mm(hid[q % 2][:, 0:E0], gt1[:, tt, g * P:(g + 1) * P], w10[:, g, :],
                           start=True, stop=True).then_inc(c1_mm, 1)
                    if 1 <= q <= Q0:
                        r = q - 1
                        tt, g = r // G0, r % G0
                        pe.wait_ge(c1_relu, r + 1)
                        need(pe, g2_copied, r)
                        for c in range(2):
                            last = mm(turn[:, c * P:(c + 1) * P], h10[:, r % 2, c * P:(c + 1) * P],
                                      ma[:, tt, g, :], start=True, stop=True)
                        last.then_inc(g2_mm, 1)
                    if q >= 2:
                        r = q - 2
                        g = r % G0
                        pe.wait_ge(g2_copied, r + 1)
                        need(pe, out_scaled, r)
                        for c in range(2):
                            last = mm(mlp[:, 0:D], gt2[:, r % 2, c * P:(c + 1) * P], w20[:, g, c, :],
                                      start=(c == 0), stop=(c == 1))
                        last.then_inc(out_mm, 1)

            def split_mm(dst, sH, sL, mH, mL, start, stop):
                mm(dst, sH, mH, start=start, stop=False)
                mm(dst, sH, mL, start=False, stop=False)
                return mm(dst, sL, mH, start=False, stop=stop)

            def a_tile(graph, acc, which, H, L, j, last_stop):
                if j % HB == 0:
                    pe.wait_ge(vH[which], cnt(graph, 2, j // HB + 1))
                    pe.wait_ge(vL[which], cnt(graph, 2, j // HB + 1))
                for g in range(2):
                    last = split_mm(acc[g][:, :], blk(H, j), blk(L, j), adjH[:, tile_cols(graph, j, g * HALF, HALF)],
                                    adjL[:, tile_cols(graph, j, g * HALF, HALF)], j == 0, last_stop and j == NB - 1)
                    if last_stop and j == NB - 1 and which == 2:
                        last.then_inc(a2_mm, 1)
                return last

            def phase_p(b, p):
                if p is not None:
                    for g in range(2):
                        pe.wait_ge(nb_copied if g == 0 else nb_copied2, cnt(p, 1, 1))
                        for k in range(HB):
                            last = mm(blk(hid[g], k), blk(colT, g * HB + k), wneigh[:, :], start=True, stop=True)
                        last.then_inc(p2_mm, 1)
                if b is not None:
                    for j in range(NB):
                        pe.wait_ge(lo_ready, cnt(b, NB, j + 1))
                        if j < NB - 1:
                            a_tile(b, acc12, 1, v1H, v1L, j, False)
                        if j == NB - 3:
                            pe.wait_ge(summed, cnt(b, 2 * (NB - 1), 2 * (NB - 1)))
                            for k in range(NB):
                                last = mm(acc3[0][:, k:k + 1], blk(rowsum, k), ones[:, :], start=True, stop=True)
                            last.then_inc(rs_mm, 1)
                    for g in range(2):
                        cols = tile_cols(b, NB - 1, g * HALF, HALF)
                        split_mm(acc12[g][:, :], blk(v1H, NB - 1), blk(v1L, NB - 1), adjH[:, cols], adjL[:, cols],
                                 False, False)
                        for k in range(HB):
                            n = g * HB + k
                            last = split_mm(blk(acc12[g], k), blk(v1H, n), blk(v1L, n), epsH[:, :], epsL[:, :],
                                            False, k == HB - 1)
                        last.then_inc(a1_mm, 1)

            def phase_q(b, p):
                for s in range(NB + 3):
                    if b is not None and s < NB:
                        if s % HB == 0:
                            pe.wait_ge(agg_copied if s == 0 else agg_copied2, cnt(b, 1, 1))
                        if s >= 2:
                            pe.wait_ge(weighted, cnt(b, NB, s - 1))
                            pe.wait_ge(squared, cnt(b, NB, s - 1))
                        elif p is not None:
                            pe.wait_ge(z_done, cnt(p, 2, s + 1))
                        mm(hid[s % 2][:, :], blk(colT, s), w1[:, :], start=True, stop=False)
                        mm(hid[s % 2][:, :], onesR[:, :], b1R[:, :], start=False, stop=True).then_inc(w1_mm, 1)
                    if p is not None and s in (2, 4):
                        layer3_turn(b, p, s // 2 - 1)
                    if p is not None and s in (3, 5):
                        layer3_transform(p, s // 2 - 1)
                    if p is not None and b is not None and s >= NB:
                        a3_tiles(p, s - NB, s - NB + 1)
                    if b is not None and 2 <= s <= NB + 1:
                        k = s - 2
                        pe.wait_ge(silu_done, cnt(b, NB, k + 1))
                        if k >= 1:
                            pe.wait_ge(sT_copied, cnt(b, NB, k))
                        elif p is not None:
                            pe.wait_ge(p1_copied, cnt(p, 2, 1))
                        for h in range(KH):
                            last = nc.tensor.transpose(blk(turn, h), blk(u[k % 2], h), ident[:, :])
                        last.then_inc(turn_mm, 1)
                    if b is not None and s >= 3:
                        k = s - 3
                        pe.wait_ge(sT_copied, cnt(b, NB, k + 1))
                        if k >= 1:
                            pe.wait_ge(x1_done, cnt(b, NB, k))
                        elif p is not None:
                            pe.wait_ge(p1_copied, cnt(p, 2, 2))
                        for h in range(KH):
                            last = mm(mlp[:, 0:D], blk(sT, h), blk(w2, h), start=(h == 0), stop=(h == KH - 1))
                        last.then_inc(w2_mm, 1)

            def a3_tiles(p, j0, j1):
                for j in range(j0, j1):
                    if j == 0:
                        pe.wait_ge(v3_steps, cnt(p, 4, 4))
                    a_tile(p, acc3, 3, v3H, v3L, j, True).then_inc(a3_tile, 1)

            def layer3_turn(b, p, g):
                pe.wait_ge(relu_done["ln3"], cnt(p, 2, g + 1))
                if g == 0:
                    if b is not None:
                        pe.wait_ge(deg_steps, cnt(b, 4, 1))
                    else:
                        pe.wait_ge(o_scaled, cnt(p - 1, 2, 2))
                else:
                    pe.wait_ge(hT_copied, cnt(p, 2, g))
                for k in range(HB):
                    last = nc.tensor.transpose(blk(acc3[0], k), blk(t[g], k), ident[:, :])
                last.then_inc(hT_mm, 1)

            def layer3_transform(p, g):
                pe.wait_ge(hT_copied, cnt(p, 2, g + 1))
                if g == 1:
                    pe.wait_ge(v3_steps, cnt(p, 4, 1))
                for k in range(HB):
                    last = mm(blk(acc3[1], k), blk(fT, k), w3[:, :], start=True, stop=True)
                last.then_inc(t3_mm, 1)

            def xn_turn(b, g):
                pe.wait_ge(xn_steps, cnt(b, 4, 2 * g + 2))
                pe.wait_ge(weighted, cnt(b, NB, NB - 1 + g))
                pe.wait_ge(squared, cnt(b, NB, NB - 1 + g))
                for k in range(HB):
                    last = nc.tensor.transpose(blk(hid[g], k), blk(xn, k), ident[:, :])
                last.then_inc(xnT_mm, 1)

            def xn_self(b, g):
                pe.wait_ge(xnT_copied, cnt(b, 2, g + 1))
                if g == 0:
                    pe.wait_ge(sT_copied, cnt(b, NB, NB))
                else:
                    pe.wait_ge(x1_done, cnt(b, NB, NB))
                for k in range(HB):
                    last = mm(blk(p1_bank[g], k), blk(fT, k), wsum[:, :], start=True, stop=True)
                last.then_inc(p1_mm, 1)

            def phase_r(b, p):
                if p is not None:
                    a3_tiles(p, 0 if b is None else 3, NB)
                if b is not None:
                    xn_turn(b, 0)
                for j in range(NB):
                    if b is not None:
                        a_tile(b, acc12, 2, v2H, v2L, j, True)
                        if j == 0:
                            xn_self(b, 0)
                    if p is not None and j == 1:
                        for g in range(2):
                            pe.wait_ge(o_copied if g == 0 else o_copied2, cnt(p, 1, 1))
                            for k in range(HB):
                                last = nc.tensor.transpose(blk(acc3[g], k), blk(colT, g * HB + k), ident[:, :])
                            last.then_inc(oT_mm, 1)
                    if b is not None and j == NB - 3:
                        xn_turn(b, 1)
                if b is not None:
                    xn_self(b, 1)

            layer0()
            phase_p(0, None)
            phase_q(0, None)
            phase_r(0, None)
            with pe.Fori(1, B) as i:
                phase_p(i, i - 1)
                phase_q(i, i - 1)
                phase_r(i, i - 1)
            phase_p(None, B - 1)
            phase_q(None, B - 1)
            phase_r(None, B - 1)

        @block.scalar
        def _(act):
            a = nc.scalar.activation

            for dst, name in ((xr, "x0"), (mask0, "mask0"), (member, "member0")):
                act.dma_start(dst[:], t_in[name]).then_inc(l0_in, 16)
            act.wait_ge(s0_pool, 1)
            for tt in range(T0):
                for q in range(4):
                    act.dma_start(adj0[q * S0:(q + 1) * S0, tt, q * S0:(q + 1) * S0],
                                  adjT_d[4 * tt + q, 0:S0, 0:S0]).then_inc(l0_in, 16)
            act.dma_start(fus[:, :], t_in["L0_gnn_fusion_w"].partition_broadcast(P)).then_inc(l0_in, 16)
            act.dma_start(ident[:, :], t_in["ident"]).then_inc(l0_in, 16)
            for dst, name in ((w10, "w10"), (w20, "w20")):
                act.dma_start(dst[:], t_in[name]).then_inc(l0_w, 16)
            act.dma_start(b10[:, :], t_in["L0_gnn_b1"].partition_broadcast(P)).then_inc(l0_w, 16)
            act.dma_start(b20[:, :], t_in["L0_gnn_b2"].partition_broadcast(P)).then_inc(l0_w, 16)
            for dst, name in ((w1, "L1_gnn_W1"), (w2, "w2"), (wneigh, "L2_gnn_W_neigh"), (wself, "L2_gnn_W_self"),
                              (w3, "w3T")):
                act.dma_start(dst[:], t_in[name]).then_inc(w_in, 16)
            for dst, name in ((wrms, "L1_gnn_rms_weight"), (b2bc, "L1_gnn_b2"), (gam, "L2_gnn_gamma"),
                              (bet, "L2_gnn_beta"), (b3bc, "L3_gnn_b"), (eps, "L1_gnn_epsilon")):
                act.dma_start(dst[:], t_in[name].partition_broadcast(P)).then_inc(w_in, 16)
            act.dma_start(b1r2[:, :], t_in["L1_gnn_b1"].partition_broadcast(2)).then_inc(w_in, 16)

            def split_hi(c, j):
                act.wait_ge(raw_in[j % RS], cnt(c, 16 * (NB // RS), 16 * (j // RS + 1)))
                if j < NB - 2 and (not isinstance(c, int) or c >= 2):
                    act.wait_ge(a3_tile, cnt(c - 2, NB, j + 1))
                if j == 0 and (not isinstance(c, int) or c >= 1):
                    act.wait_ge(deg_steps, cnt(c - 1, 4, 3))
                a(adjH[:, tile_cols(c, j, 0, N)], raw[:, j % RS, :], ACT.Copy,
                  accum_out=deg[:, NB + j:NB + j + 1]).then_inc(hi_ready, 1)

            def layer0():
                act.wait_ge(s0_dve, 5)
                a(fex[:, :], fus[:, :], ACT.Exp, bias=fmx[:, 1:2], accum_out=fsum[:, 0:1]).then_inc(s0_act, 1)
                act.wait_ge(s0_dve, 8)
                a(h0[:].rearrange("p t d -> p (t d)"), h0[:].rearrange("p t d -> p (t d)"), ACT.Relu).then_inc(s0_act, 1)
                act.wait_ge(s0_pe, 2)
                for tt in range(T0):
                    a(gt1[:, tt, 0:HALF], acc3[tt][:, :], ACT.Copy)
                    a(gt1[:, tt, HALF:], hid[tt][:, 0:P], ACT.Copy).then_inc(s0_act, 1)
                for q in range(T0 * G0):
                    act.wait_ge(c1_scaled, q + 1)
                    a(h10[:, q % 2, :], h10[:, q % 2, :], ACT.Relu).then_inc(c1_relu, 1)
                    act.wait_ge(g2_mm, q + 1)
                    need(act, out_mm, q - 1)
                    a(gt2[:, q % 2, :], turn[:, 0:E0], ACT.Copy).then_inc(g2_copied, 1)
                    if q < NB:
                        split_hi(0, q)

            def relu(kind, graph, g):
                act.wait_ge(ln_rstd[kind], cnt(graph, 2, g + 1))
                dst = t1[g] if kind == "ln1" else t[g]
                for k in range(HB):
                    last = a(blk(dst, k), xcols(graph, g * HB + k, 1), ACT.Relu, scale=rstd[kind][g][:, k:k + 1],
                             bias=shift[kind][g][:, k:k + 1])
                last.then_inc(relu_done[kind], 1)

            def v_hi(which, H, graph, g, ready, value):
                act.wait_ge(ready, value)
                a(H[:, g * HALF:(g + 1) * HALF], (t1 if which == 1 else t)[g][:, :], ACT.Copy).then_inc(vH[which], 1)

            def phase_p(b, p):
                if p is not None:
                    act.wait_ge(nb_copied2, cnt(p, 1, 1))
                    for g in range(2):
                        act.wait_ge(p1_mm, cnt(p, 2, g + 1))
                        a(z[g][:, :], p1_bank[g][:, :], ACT.Copy).then_inc(p1_copied, 1)
                    if b is not None:
                        for j in range(NB - 2, NB):
                            split_hi(b, j)
                    for g in range(2):
                        act.wait_ge(xz_done, cnt(p, 2, g + 1))
                        a(z[g][:, :], z[g][:, :], ACT.Abs).then_inc(sp_steps, 1)
                    for g in range(2):
                        act.wait_ge(sp_steps, cnt(p, 6, 1 + g))
                        a(z[g][:, :], z[g][:, :], ACT.Exp, scale=-1.0).then_inc(sp_steps, 1)
                    for g in range(2):
                        act.wait_ge(sp_steps, cnt(p, 6, 3 + g))
                        a(z[g][:, :], z[g][:, :], ACT.Ln, bias=1.0).then_inc(sp_steps, 1)
                if b is not None:
                    act.wait_ge(a1_mm, cnt(b, 2, 1))
                    a(colT[:, 0:HALF], acc12[0][:, :], ACT.Copy).then_inc(agg_copied, 1)
                if p is not None:
                    relu("ln3", p, 0)

            def phase_q(b, p, c):
                for s in range(NB + 2):
                    if b is not None and s < NB:
                        act.wait_ge(w1_mm, cnt(b, NB, s + 1))
                        if s >= 2:
                            act.wait_ge(msq, cnt(b, NB, s - 1))
                        if not isinstance(b, int) or b or s:
                            act.wait_ge(squared, cnt(b, NB, s))
                        a(junk[:, :], hid[s % 2][:, :], ACT.Square, scale=HID ** -0.5,
                          accum_out=ss[:, s % 2:s % 2 + 1]).then_inc(squared, 1)
                    if p is not None and s in (2, 4):
                        turn3_copy(p, s // 2 - 1)
                    if b is not None and 1 <= s <= NB:
                        k = s - 1
                        act.wait_ge(rms, cnt(b, NB, k + 1))
                        act.wait_ge(weighted, cnt(b, NB, k + 1))
                        a(u[k % 2][:, :], u[k % 2][:, :], ACT.Silu, scale=rrms[:, k % 2:k % 2 + 1]).then_inc(silu_done, 1)
                    if p is not None and s in (4, 6):
                        g = s // 2 - 2
                        v_hi(3, v3H, p, g, v3_steps, cnt(p, 4, 2 * g + 2))
                    if b is not None and 2 <= s <= NB + 1:
                        k = s - 2
                        act.wait_ge(turn_mm, cnt(b, NB, k + 1))
                        if k >= 1:
                            act.wait_ge(w2_mm, cnt(b, NB, k))
                        a(sT[:, :], turn[:, :], ACT.Copy).then_inc(sT_copied, 1)
                    if p is not None and s == 2:
                        relu("ln3", p, 1)
                    if b is not None and s == NB:
                        relu("ln2a", b, 0)

            def turn3_copy(p, g):
                act.wait_ge(hT_mm, cnt(p, 2, g + 1))
                if g == 1:
                    act.wait_ge(t3_mm, cnt(p, 2, 1))
                else:
                    act.wait_ge(p1_mm, cnt(p, 2, 2))
                a(fT[:, :], acc3[0][:, :], ACT.Copy).then_inc(hT_copied, 1)

            def phase_r(b, p, c):
                if c is not None:
                    for j in range(3):
                        split_hi(c, j)
                if b is not None:
                    relu("ln2a", b, 1)
                    v_hi(2, v2H, b, 0, v2_scaled, cnt(b, 2, 1))
                if c is not None:
                    split_hi(c, 3)
                if p is not None:
                    act.wait_ge(a3_tile, cnt(p, NB, NB))
                    if b is not None:
                        act.wait_ge(w1_mm, cnt(b, NB, NB))
                    a(colT[:, 0:HALF], acc3[0][:, :], ACT.Copy).then_inc(o_copied, 1)
                if b is not None:
                    act.wait_ge(xnT_mm, cnt(b, 2, 1))
                    if p is not None:
                        act.wait_ge(t3_mm, cnt(p, 2, 2))
                    a(fT[:, :], hid[0][:, :], ACT.Copy).then_inc(xnT_copied, 1)
                if b is not None:
                    v_hi(2, v2H, b, 1, v2_scaled, cnt(b, 2, 2))
                if c is not None:
                    for j in range(4, NB - 2):
                        split_hi(c, j)
                    for g in range(2):
                        relu("ln1", c, g)
                    for g in range(2):
                        v_hi(1, v1H, c, g, relu_done["ln1"], cnt(c, 2, g + 1))
                if b is not None:
                    act.wait_ge(xnT_mm, cnt(b, 2, 2))
                    act.wait_ge(p1_mm, cnt(b, 2, 1))
                    a(fT[:, :], hid[1][:, :], ACT.Copy).then_inc(xnT_copied, 1)
                    act.wait_ge(a2_mm, cnt(b, 2, 1))
                    if p is not None:
                        act.wait_ge(oT_mm, cnt(p, 2, 2))
                    a(colT[:, 0:HALF], acc12[0][:, :], ACT.Copy).then_inc(nb_copied, 1)

            layer0()
            for g in range(2):
                relu("ln1", 0, g)
                v_hi(1, v1H, 0, g, relu_done["ln1"], cnt(0, 2, g + 1))
            phase_p(0, None)
            phase_q(0, None, 1)
            phase_r(0, None, 1)
            with act.Fori(1, B - 1) as i:
                phase_p(i, i - 1)
                phase_q(i, i - 1, i + 1)
                phase_r(i, i - 1, i + 1)
            phase_p(B - 1, B - 2)
            phase_q(B - 1, B - 2, None)
            phase_r(B - 1, B - 2, None)
            phase_p(None, B - 1)
            phase_q(None, B - 1, None)
            phase_r(None, B - 1, None)

        @block.vector
        def _(dve):
            v = nc.vector

            def setup():
                v.memset(ones[:, :], 1.0)
                v.memset(rms_eps[:, :], 1e-6)
                v.memset(power[:, :], -0.5).then_inc(const_ready, 1)

            def layer0():
                dve.wait_ge(l0_in, 16 * 13)
                i2 = ident[:, :].unsqueeze(1).broadcast_to([P, T0, P])
                v.tensor_tensor(adj0[:], adj0[:], i2, ALU.add).then_inc(s0_dve, 1)
                dve.wait_ge(s0_dve, 1)
                for tt in range(T0):
                    last = v.tensor_tensor(ma[:, tt, :, :], mask0[:], adj0[:, tt, :].unsqueeze(1)
                                           .broadcast_to([P, G0, P]), ALU.mult)
                last.then_inc(s0_dve, 1)
                v.tensor_reduce(fmx[:, 0:1], fus[:, :], AX.X, ALU.max).then_inc(s0_dve, 1)
                for tt in range(T0):
                    last = v.bn_stats(st0[:, tt, :], xr[:, tt, :])
                last.then_inc(s0_dve, 1)
                dve.wait_ge(s0_dve, 4)
                for tt in range(T0):
                    v.bn_aggr(mv0[:, tt, :], st0[:, tt, :])
                v.tensor_scalar(fmx[:, 1:2], fmx[:, 0:1], -1.0, None, ALU.mult).then_inc(s0_dve, 1)
                dve.wait_ge(s0_dve, 5)
                v.tensor_scalar(ve0[:, :], mv0[:, :, 1], 1e-5, None, ALU.add).then_inc(s0_dve, 1)
                dve.wait_ge(s0_pe, 1)
                v.tensor_scalar(dg0[:, 0, :], acc12[0][:, 0:T0 * G0], 0.0, None, ALU.is_equal)
                v.tensor_scalar(dg0[:, 1, :], acc12[0][:, 0:T0 * G0], 0.0, None, ALU.not_equal).then_inc(s0_own, 1)
                dve.wait_ge(s0_own, 1)
                v.tensor_tensor(dg0[:, 2, :], acc12[0][:, 0:T0 * G0], dg0[:, 0, :], ALU.add).then_inc(s0_dve, 1)
                dve.wait_ge(s0_pool, 2)
                for tt in range(T0):
                    last = v.tensor_scalar(h0[:, tt, :], xr[:, tt, :], mv0[:, tt, 0:1], rs0[:, tt:tt + 1],
                                           ALU.subtract, ALU.mult)
                last.then_inc(s0_dve, 1)
                dve.wait_ge(s0_pool, 3)
                v.tensor_tensor(di0[:, :], dg0[:, 3, :], dg0[:, 1, :], ALU.mult).then_inc(s0_own, 1)
                dve.wait_ge(s0_own, 2)
                for q in range(T0 * G0):
                    m = ma[:, q // G0, q % G0, :]
                    last = v.tensor_scalar(m, m, di0[:, q:q + 1], None, ALU.mult)
                last.then_inc(s0_dve, 1)
                dve.wait_ge(s0_act, 1)
                v.reciprocal(fsum[:, 1:2], fsum[:, 0:1]).then_inc(s0_own, 1)
                dve.wait_ge(s0_own, 3)
                v.scalar_tensor_tensor(cw[:, :], fex[:, :], fsum[:, 1:2], member[:, :], ALU.mult, ALU.mult
                                       ).then_inc(s0_dve, 1)
                dve.wait_ge(s0_dve, 10)
                dve.wait_ge(l0_w, 16 * 4)
                Q0 = T0 * G0
                for q in range(Q0 + 2):
                    if q < Q0:
                        g = q % G0
                        dve.wait_ge(c1_mm, q + 1)
                        need(dve, g2_mm, q - 1)
                        v.scalar_tensor_tensor(h10[:, q % 2, :], hid[q % 2][:, 0:E0], di0[:, q:q + 1],
                                               b10[:, g * E0:(g + 1) * E0], ALU.mult, ALU.add
                                               ).then_inc(c1_scaled, 1)
                    if q >= 2:
                        r = q - 2
                        tt, g = r // G0, r % G0
                        dve.wait_ge(out_mm, r + 1)
                        v.scalar_tensor_tensor(o0[:, 0, :], mlp[:, 0:D], di0[:, r:r + 1],
                                               b20[:, g * D:(g + 1) * D], ALU.mult, ALU.add).then_inc(out_scaled, 1)
                        dve.wait_ge(out_scaled, r + 1)
                        v.tensor_scalar(o0[:, 1, :], o0[:, 0, :], 0.0, cw[:, g:g + 1], ALU.max, ALU.mult
                                        ).then_inc(out_weighted, 1)
                        dve.wait_ge(out_weighted, r + 1)
                        v.tensor_tensor(xr[:, tt, :], xr[:, tt, :], o0[:, 1, :], ALU.add).then_inc(x0_added, 1)
                        dve.wait_ge(x0_added, r + 1)
                    if 1 <= q <= NB:
                        split_lo(0, q - 1)

            def weights():
                dve.wait_ge(w_in, 16 * 12)
                v.tensor_tensor(wsum[:, :], wself[:, :], wneigh[:, :], ALU.add)
                v.tensor_scalar(epsI[:, :], ident[:, :], eps[:, 0:1], None, ALU.mult)
                v.tensor_copy(b1hi[:, :], b1r2[:, :])
                v.tensor_copy(onesR[:, :], ones[0:2, :].broadcast_to([2, P])).then_inc(const_ready, 1)
                dve.wait_ge(const_ready, 2)
                v.tensor_copy(epsH[:, :], epsI[:, :])
                v.tensor_tensor(b1lo[:, :], b1r2[:, :], b1hi[:, :].bitcast(F32), ALU.subtract).then_inc(const_ready, 1)
                dve.wait_ge(const_ready, 3)
                v.tensor_tensor(epsL[:, :], epsI[:, :], epsH[:, :].bitcast(F32), ALU.subtract)
                v.tensor_scalar(b1lo[:, :], b1lo[:, :], ident[0:2, 1:2], None, ALU.mult).then_inc(const_ready, 1)
                dve.wait_ge(const_ready, 4)
                v.scalar_tensor_tensor(b1R[:, :], b1hi[:, :].bitcast(F32), ident[0:2, 0:1], b1lo[:, :],
                                       ALU.mult, ALU.add).then_inc(const_ready, 1)

            def split_lo(c, j):
                dve.wait_ge(hi_ready, cnt(c, NB, j + 1))
                if j < RS and j % 2:
                    dve.wait_ge(summed, cnt(c, 2 * (NB - 1), 2 * j))
                cols = tile_cols(c, j, 0, N)
                v.tensor_tensor(adjL[:, cols], raw[:, j % RS, :], adjH[:, cols].bitcast(F32), ALU.subtract
                                ).then_inc(lo_ready, 1)

            def stats(kind, graph, g, source):
                steps = ln_steps[kind]
                v.tensor_copy(tick[:, 0:1], power[:, 0:1])
                for k in range(HB):
                    last = v.bn_stats(stat6[:, k, :], source(k))
                last.then_inc(steps, 1)
                dve.wait_ge(steps, cnt(graph, 6, 3 * g + 1))
                v.tensor_copy(tick[:, 1:2], power[:, 0:1])
                for k in range(HB):
                    last = v.bn_aggr(mv[kind][g][:, k, :], stat6[:, k, :])
                last.then_inc(steps, 1)
                dve.wait_ge(steps, cnt(graph, 6, 3 * g + 2))
                v.tensor_scalar(negmean[kind][g][:, :], mv[kind][g][:, :, 0], -1.0, None, ALU.mult)
                v.tensor_scalar(veps[kind][g][:, :], mv[kind][g][:, :, 1], 1e-5, None, ALU.add).then_inc(steps, 1)

            def v_lo(which, H, L, graph, g):
                dve.wait_ge(vH[which], cnt(graph, 2, g + 1))
                cols = slice(g * HALF, (g + 1) * HALF)
                v.tensor_tensor(L[:, cols], (t1 if which == 1 else t)[g][:, :], H[:, cols].bitcast(F32), ALU.subtract).then_inc(vL[which], 1)

            def xsrc(graph, g):
                return lambda k: xcols(graph, g * HB + k, 1)

            def tsrc(g):
                return lambda k: blk(t[g], k)

            def degrees(b):
                dve.wait_ge(rs_mm, cnt(b, 1, 1))
                v.tensor_copy(deg[:, 0:NB], acc3[0][:, 0:NB]).then_inc(deg_steps, 1)
                dve.wait_ge(deg_steps, cnt(b, 4, 1))
                dve.wait_ge(hi_ready, cnt(b, NB, NB))
                v.tensor_scalar(dz[:, :], deg[:, :], 0.0, None, ALU.is_equal)
                v.tensor_scalar(dnz[:, 0:NB], deg[:, 0:NB], 0.0, None, ALU.not_equal)
                v.tensor_scalar(dnz[:, NB:], deg[:, NB:], 0.0, -1.0, ALU.not_equal, ALU.mult).then_inc(deg_steps, 1)
                dve.wait_ge(deg_steps, cnt(b, 4, 2))
                v.tensor_tensor(dsafe[:, :], deg[:, :], dz[:, :], ALU.add).then_inc(deg_steps, 1)

            def degrees_end(b):
                dve.wait_ge(deg_pow, cnt(b, 1, 1))
                v.tensor_tensor(sc_b[:, :], dpow[:, :], dnz[:, :], ALU.mult).then_inc(deg_steps, 1)

            def phase_p(b, p, c):
                if p is not None:
                    v.tensor_copy(sc_p[:, :], sc_b[:, :]).then_inc(sc_kept, 1)
                    dve.wait_ge(sc_kept, cnt(p, 1, 1))
                    for g in range(2):
                        dve.wait_ge(p1_copied, cnt(p, 2, g + 1))
                        dve.wait_ge(p2_mm, cnt(p, 2, g + 1))
                        for k in range(HB):
                            n = g * HB + k
                            last = v.scalar_tensor_tensor(blk(z[g], k), blk(hid[g], k), sc_p[:, NB + n:NB + n + 1],
                                                          blk(z[g], k), ALU.mult, ALU.add)
                        last.then_inc(z_done, 1)
                        dve.wait_ge(z_done, cnt(p, 2, g + 1))
                        v.scalar_tensor_tensor(xcols(p, g * HB, HB), z[g][:, :], 0.0, xcols(p, g * HB, HB),
                                               ALU.max, ALU.add).then_inc(xz_done, 1)
                    if b is not None:
                        for j in range(NB - 2, NB):
                            split_lo(b, j)
                if c is not None:
                    for g in range(2):
                        stats_1(c, g)
                if b is not None:
                    degrees(b)
                if p is not None:
                    for g in range(2):
                        dve.wait_ge(sp_steps, cnt(p, 6, 5 + g))
                        v.tensor_tensor(xcols(p, g * HB, HB), xcols(p, g * HB, HB), z[g][:, :], ALU.add
                                        ).then_inc(x2_done, 1)
                        dve.wait_ge(x2_done, cnt(p, 2, g + 1))
                        stats("ln3", p, g, xsrc(p, g))
                if b is not None:
                    dve.wait_ge(a1_mm, cnt(b, 2, 2))
                    v.tensor_copy(colT[:, HALF:], acc12[1][:, :]).then_inc(agg_copied2, 1)

            def phase_q(b, p, c):
                for s in range(NB + 3):
                    if b is not None and s < NB:
                        dve.wait_ge(w1_mm, cnt(b, NB, s + 1))
                        if s >= 2:
                            dve.wait_ge(turn_mm, cnt(b, NB, s - 1))
                        dve.wait_ge(squared, cnt(b, NB, s + 1))
                        v.tensor_tensor(u[s % 2][:, :], hid[s % 2][:, :], wrms[:, :], ALU.mult).then_inc(weighted, 1)
                    if b is not None and s >= 3:
                        k = s - 3
                        dve.wait_ge(w2_mm, cnt(b, NB, k + 1))
                        if k == 0:
                            dve.wait_ge(xb2, cnt(b, 1, 1))
                        v.tensor_tensor(xcols(b, k, 1), xcols(b, k, 1), mlp[:, 0:D], ALU.add).then_inc(x1_done, 1)
                    if p is not None and s in (3, 5):
                        g = s // 2 - 1
                        dve.wait_ge(t3_mm, cnt(p, 2, g + 1))
                        v.tensor_tensor(by_block(t[g][:, :]), by_block(acc3[1][:, :]), over_blocks(b3bc), ALU.add
                                        ).then_inc(v3_steps, 1)
                        dve.wait_ge(v3_steps, cnt(p, 4, 2 * g + 1))
                        for k in range(HB):
                            n = g * HB + k
                            last = v.tensor_scalar(blk(t[g], k), blk(t[g], k), sc_p[:, n:n + 1], None, ALU.mult)
                        last.then_inc(v3_steps, 1)
                    if p is not None and s in (4, 6):
                        v_lo(3, v3H, v3L, p, s // 2 - 2)
                    if b is not None and s == HB + 2:
                        dve.wait_ge(x1_done, cnt(b, NB, HB))
                        stats("ln2a", b, 0, xsrc(b, 0))
                    if b is not None and s == NB + 1:
                        xn_norm(b, 0)

            def xn_norm(b, g):
                dve.wait_ge(relu_done["ln2a"], cnt(b, 2, g + 1))
                stats("ln2b", b, g, tsrc(g))
                for k in range(HB):
                    last = v.scalar_tensor_tensor(blk(t[g], k), blk(t[g], k), mv["ln2b"][g][:, k, 0:1], gam[:, :],
                                                  ALU.subtract, ALU.mult)
                last.then_inc(xn_steps, 1)

            def xn_end(b, g):
                dve.wait_ge(pow_done["ln2b"], cnt(b, 2, g + 1))
                dve.wait_ge(xn_steps, cnt(b, 4, 2 * g + 1))
                if g == 1:
                    dve.wait_ge(xnT_mm, cnt(b, 2, 1))
                    dve.wait_ge(v2_scaled, cnt(b, 2, 1))
                for k in range(HB):
                    last = v.scalar_tensor_tensor(blk(xn, k), blk(t[g], k), rstd["ln2b"][g][:, k:k + 1], bet[:, :],
                                                  ALU.mult, ALU.add)
                last.then_inc(xn_steps, 1)

            def xn_scale(b, g):
                dve.wait_ge(xn_steps, cnt(b, 4, 2 * g + 2))
                for k in range(HB):
                    n = g * HB + k
                    last = v.tensor_scalar(blk(t[g], k), blk(xn, k), sc_b[:, n:n + 1], None, ALU.mult)
                last.then_inc(v2_scaled, 1)

            def output(b, p, g):
                dve.wait_ge(oT_mm, cnt(p, 2, g + 1))
                if b is not None:
                    dve.wait_ge(turn_mm, cnt(b, NB, NB))
                s_in = sc_p[:, g * HB:(g + 1) * HB].unsqueeze(2).broadcast_to([P, HB, D])
                v.scalar_tensor_tensor(by_block(z[g][:, :]), by_block(acc3[g][:, :]), 0.0, s_in,
                                       ALU.max, ALU.mult).then_inc(o_scaled, 1)
                dve.wait_ge(o_scaled, cnt(p, 2, g + 1))
                v.tensor_tensor(xcols(p, g * HB, HB), xcols(p, g * HB, HB), z[g][:, :], ALU.add
                                ).then_inc(x3_done, 1)

            def phase_r(b, p, c):
                if b is not None:
                    dve.wait_ge(x1_done, cnt(b, NB, NB))
                    stats("ln2a", b, 1, xsrc(b, 1))
                    degrees_end(b)
                    xn_end(b, 0)
                    xn_scale(b, 0)
                if c is not None:
                    split_lo(c, 0)
                if b is not None:
                    v_lo(2, v2H, v2L, b, 0)
                if c is not None:
                    split_lo(c, 1)
                if b is not None:
                    xn_norm(b, 1)
                if p is not None:
                    dve.wait_ge(a3_tile, cnt(p, NB, NB))
                    if b is not None:
                        dve.wait_ge(w1_mm, cnt(b, NB, NB))
                    v.tensor_copy(colT[:, HALF:], acc3[1][:, :]).then_inc(o_copied2, 1)
                if b is not None:
                    xn_end(b, 1)
                    xn_scale(b, 1)
                if c is not None:
                    split_lo(c, 2)
                if b is not None:
                    v_lo(2, v2H, v2L, b, 1)
                if c is not None:
                    split_lo(c, 3)
                if p is not None:
                    output(b, p, 0)
                if c is not None:
                    split_lo(c, 4)
                if p is not None:
                    output(b, p, 1)
                if c is not None:
                    split_lo(c, 5)
                    v_lo(1, v1H, v1L, c, 0)
                    v_lo(1, v1H, v1L, c, 1)
                if b is not None:
                    dve.wait_ge(a2_mm, cnt(b, 2, 2))
                    if p is not None:
                        dve.wait_ge(oT_mm, cnt(p, 2, 2))
                    v.tensor_copy(colT[:, HALF:], acc12[1][:, :]).then_inc(nb_copied2, 1)

            def stats_1(c, g):
                if g == 0:
                    dve.wait_ge(x0_in, cnt(c, 16, 16))
                stats("ln1", c, g, xsrc(c, g))

            setup()
            layer0()
            weights()
            for g in range(2):
                stats_1(0, g)
            for g in range(2):
                v_lo(1, v1H, v1L, 0, g)
            phase_p(0, None, 1)
            phase_q(0, None, 1)
            phase_r(0, None, 1)
            with dve.Fori(1, B - 1) as i:
                phase_p(i, i - 1, i + 1)
                phase_q(i, i - 1, i + 1)
                phase_r(i, i - 1, i + 1)
            phase_p(B - 1, B - 2, None)
            phase_q(B - 1, B - 2, None)
            phase_r(B - 1, B - 2, None)
            phase_p(None, B - 1, None)
            phase_q(None, B - 1, None)
            phase_r(None, B - 1, None)

        @block.gpsimd
        def _(pool):
            gp = nc.gpsimd

            def pw(dst, src, n):
                return gp.tensor_tensor(dst, src, power[:, 0:n], ALU.pow)

            def add_rows(c, j):
                for h in range(2):
                    add_half(c, j, h)

            def add_half(c, j, h):
                cols = slice(h * HALF, (h + 1) * HALF)
                if h == 0:
                    pool.wait_ge(raw_in[j % RS], cnt(c, 16 * (NB // RS), 16 * (j // RS + 1)))
                if j == 1:
                    if h == 0:
                        pool.wait_ge(raw_in[0], cnt(c, 16 * (NB // RS), 16))
                        if not isinstance(c, int) or c >= 1:
                            pool.wait_ge(rs_mm, cnt(c - 1, 1, 1))
                    first = raw[:, 0, cols]
                else:
                    pool.wait_ge(summed, cnt(c, 2 * (NB - 1), 2 * (j - 2) + h + 1))
                    first = rowsum[:, cols]
                gp.tensor_tensor(rowsum[:, cols], first, raw[:, j % RS, cols], ALU.add).then_inc(summed, 1)

            def rstd_of(kind, graph, g):
                pool.wait_ge(ln_steps[kind], cnt(graph, 6, 3 * g + 3))
                pw(rstd[kind][g][:, :], veps[kind][g][:, :], HB).then_inc(pow_done[kind], 1)
                if kind == "ln2b":
                    return
                pool.wait_ge(pow_done[kind], cnt(graph, 2, g + 1))
                gp.tensor_tensor(shift[kind][g][:, :], negmean[kind][g][:, :], rstd[kind][g][:, :], ALU.mult
                                 ).then_inc(ln_rstd[kind], 1)

            def phase_p(b, p, c):
                if b is not None and p is not None:
                    for j in range(NB - 2, NB):
                        add_rows(b, j)
                if c is not None:
                    rstd_of("ln1", c, 0)
                    rstd_of("ln1", c, 1)
                if p is not None:
                    rstd_of("ln3", p, 0)
                    rstd_of("ln3", p, 1)

            def phase_q(b, p, c):
                for s in range(NB):
                    if b is not None:
                        pool.wait_ge(squared, cnt(b, NB, s + 1))
                        if s >= 2:
                            pool.wait_ge(silu_done, cnt(b, NB, s - 1))
                        e = s % 2
                        gp.tensor_tensor(sse[:, e:e + 1], ss[:, e:e + 1], rms_eps[:, :], ALU.add).then_inc(msq, 1)
                        pool.wait_ge(msq, cnt(b, NB, s + 1))
                        pw(rrms[:, e:e + 1], sse[:, e:e + 1], 1).then_inc(rms, 1)
                    if c is not None and 1 <= s <= 2 * (RS - 1):
                        add_half(c, (s + 1) // 2, (s + 1) % 2)
                if b is not None:
                    rstd_of("ln2a", b, 0)
                    pool.wait_ge(deg_steps, cnt(b, 4, 3))
                    pw(dpow[:, :], dsafe[:, :], 2 * NB).then_inc(deg_pow, 1)

            def phase_r(b, p, c):
                if b is not None:
                    rstd_of("ln2b", b, 0)
                    rstd_of("ln2a", b, 1)
                    rstd_of("ln2b", b, 1)
                if c is not None:
                    for j in range(RS, NB - 2):
                        add_rows(c, j)
                    plus_b2(c)

            def plus_b2(c):
                pool.wait_ge(relu_done["ln1"], cnt(c, 2, 2))
                gp.tensor_tensor(by_block(xcols(c, 0, NB)), by_block(xcols(c, 0, NB)), over_blocks(b2bc, NB), ALU.add
                                 ).then_inc(xb2, 1)

            gp.memset(adj0[:], 0.0).then_inc(s0_pool, 1)
            pool.wait_ge(const_ready, 1)
            pool.wait_ge(s0_dve, 6)
            pw(rs0[:, :], ve0[:, :], T0).then_inc(s0_pool, 1)
            pool.wait_ge(s0_dve, 7)
            pw(dg0[:, 3, :], dg0[:, 2, :], T0 * G0).then_inc(s0_pool, 1)
            for j in range(1, NB):
                add_rows(0, j)
            rstd_of("ln1", 0, 0)
            rstd_of("ln1", 0, 1)
            plus_b2(0)
            phase_p(0, None, 1)
            phase_q(0, None, 1)
            phase_r(0, None, 1)
            with pool.Fori(1, B - 1) as i:
                phase_p(i, i - 1, i + 1)
                phase_q(i, i - 1, i + 1)
                phase_r(i, i - 1, i + 1)
            phase_p(B - 1, B - 2, None)
            phase_q(B - 1, B - 2, None)
            phase_r(B - 1, B - 2, None)
            phase_p(None, B - 1, None)


def kernel(**inputs):
    import concourse.bacc as bacc
    from concourse.bass_utils import run_bass_kernel_spmd as run

    def laid(a):
        return np.ascontiguousarray(a)

    x, adj = np.asarray(inputs["x"]), np.asarray(inputs["adj"])
    node = np.arange(P) % S0
    graph = np.arange(P) // S0
    member = np.stack([np.isin(node, g) for g in GROUPS], 1)
    mask = member[:, None, :] & member[None, :, :] & (graph[:, None] == graph[None, :])[:, :, None]
    arrays = {
        "x": x,
        "adjT": adj.transpose(0, 2, 1),
        "x0": x[:, 0:S0].reshape(T0, P, D).transpose(1, 0, 2),
        "mask0": mask.transpose(0, 2, 1).astype(np.float32),
        "member0": member.astype(np.float32),
        "ident": np.eye(P, dtype=np.float32),
        "w10": np.asarray(inputs["L0_gnn_W1"]).transpose(1, 0, 2),
        "w20": np.asarray(inputs["L0_gnn_W2"]).reshape(G0, 2, P, D).transpose(2, 0, 1, 3),
        "L0_gnn_b1": np.asarray(inputs["L0_gnn_b1"]).reshape(-1),
        "L0_gnn_b2": np.asarray(inputs["L0_gnn_b2"]).reshape(-1),
        "w2": np.asarray(inputs["L1_gnn_W2"]).reshape(KH, P, D).transpose(1, 0, 2).reshape(P, KH * D),
        "w3T": np.asarray(inputs["L3_gnn_W"]).T,
        "L1_gnn_epsilon": np.asarray(inputs["L1_gnn_epsilon"]).reshape(1),
    }
    for name in ("L0_gnn_fusion_w", "L1_gnn_W1", "L1_gnn_b1", "L1_gnn_rms_weight", "L1_gnn_b2", "L2_gnn_gamma",
                 "L2_gnn_beta", "L2_gnn_W_self", "L2_gnn_W_neigh", "L3_gnn_b"):
        arrays[name] = np.asarray(inputs[name])
    nc = bacc.Bacc("TRN2", target_bir_lowering=False, num_devices=1, dynamic_dma_scratch_size=1024)
    arrays = {f"in_{k}": laid(a) for k, a in arrays.items()}
    t_in = {k[3:]: nc.dram_tensor(k, a.shape, F32, kind="ExternalInput").ap() for k, a in arrays.items()}
    out = nc.dram_tensor("out", x.shape, F32, kind="ExternalOutput").ap()
    build(nc, t_in, out)
    return run(nc, [arrays], core_ids=[0]).results[0]["out"]
```

```python
from contextlib import ExitStack

import numpy as np

import concourse.bass as bass
from concourse import mybir

B, N, D, HID = 8, 1024, 128, 512
P = 128
NB = N // P
HB = NB // 2
HALF = N // 2
KH = HID // P
G0, T0, S0 = 5, 2, 32
E0 = 256
N0 = 25
XS = 3
RS = 4
GROUPS = [list(range(25)), [0, 1, 2, 3, 4, 5, 6, 7, 8], [0, 9, 10, 11, 12, 13, 14], [6, 7, 8, 12, 13, 14],
          [3, 4, 5, 9, 10, 11]]

F32 = mybir.dt.float32
F32R = mybir.dt.float32r
ALU = mybir.AluOpType
ACT = mybir.ActivationFunctionType
AX = mybir.AxisListType


def cnt(graph, per_graph, c):
    return graph * per_graph + c


def need(eng, sem, value):
    if isinstance(value, int) and value <= 0:
        return
    eng.wait_ge(sem, value)


def build(nc, t_in, out):
    x_d, adjT_d = t_in["x"], t_in["adjT"]
    x0_d = nc.dram_tensor("x_layer0", (T0, P, D), F32).ap()

    with ExitStack() as ctx:
        def sb(name, shape, dt=F32, where=ctx):
            return where.enter_context(nc.sbuf_tensor(name, shape, dt))

        def sem(name):
            return ctx.enter_context(nc.semaphore(name))

        def bank(name):
            return ctx.enter_context(nc.psum_tensor(name, [P, HALF], F32))

        acc12 = [bank("acc12_0"), bank("acc12_1")]
        acc3 = [bank("acc3_0"), bank("acc3_1")]
        hid = [bank("hid_0"), bank("hid_1")]
        turn = bank("turn")
        mlp = bank("mlp")
        p1_bank = [turn, mlp]

        X = sb("X", [P, XS * N])
        raw = sb("raw", [P, RS, N])
        rowsum = sb("rowsum", [P, N])
        v1H, v1L = v3H, v3L = sb("v13H", [P, N], F32R), sb("v13L", [P, N], F32R)
        aggH, aggL = v2H, v2L = sb("v2H", [P, N], F32R), sb("v2L", [P, N], F32R)
        colT = sb("colT", [P, N])
        xn = sb("xn", [P, HALF])
        fT = sb("fT", [P, HALF])
        t = [sb("t_0", [P, HALF]), sb("t_1", [P, HALF])]
        t1 = [sb("t1_0", [P, HALF]), sb("t1_1", [P, HALF])]
        u = [sb("u_0", [P, HALF]), sb("u_1", [P, HALF])]
        sT = sb("sT", [P, HALF])
        z = u
        w1H, w1L = sb("w1H", [P, HID], F32R), sb("w1L", [P, HID], F32R)
        weights_in = sb("weights_in", [P, HID + 2 * D])
        w2 = weights_in[:, 0:HID]
        wneigh, w3 = weights_in[:, HID:HID + D], weights_in[:, HID + D:]
        wsum = sb("wsum", [P, D])
        ident = sb("ident", [P, P])
        epsH, epsL = sb("epsH", [P, P], F32R), sb("epsL", [P, P], F32R)
        rows_in = sb("rows_in", [P, HID + 4 * D + 1])
        wrms = rows_in[:, 0:HID]
        b2bc, gam, bet, b3bc = (rows_in[:, HID + k * D:HID + (k + 1) * D] for k in range(4))
        eps = rows_in[:, HID + 4 * D:]
        b1R = sb("b1R", [2, HID], F32R)
        onesR = sb("onesR", [2, P], F32R)
        ones = sb("ones", [P, 1])
        power = sb("power", [P, 16])
        stat6 = sb("stat6", [P, HB, 6])
        stat6_x1 = sb("stat6_x1", [P, HB, 6])
        ln = ["ln1", "ln2a", "ln2b", "ln3"]

        def small(name, *shape):
            return {k: [sb(f"{name}_{k}_{g}", [P, *shape]) for g in range(2)] for k in ln}
        mv, negmean, veps = small("mv", HB, 2), small("negmean", HB), small("veps", HB)
        rstd, shift = small("rstd", HB), small("shift", HB)
        tick = sb("tick", [P, 2 + NB])
        warm = sb("warm", [P, 1])
        junk = sb("junk", [P, HID], mybir.dt.bfloat16)
        ss = sb("ss", [P, 2])
        rms_eps = sb("rms_eps", [P, 1])
        sse = sb("sse", [P, 2])
        rrms = sb("rrms", [P, 2])
        deg = sb("deg", [P, 16])
        dnz = sb("dnz", [P, 16])
        dz = sb("dz", [P, 16])
        dsafe = sb("dsafe", [P, 16])
        dpow = sb("dpow", [P, 16])
        sc_b = sb("sc_b", [P, 16])
        sc_p = sb("sc_p", [P, 16])

        def sb0(name, shape, dt=F32):
            return sb(name, shape, dt, early)
        with ExitStack() as early:
            in0 = sb0("in0", [P, 2 * T0 * D + G0])
            xr, adj0 = (in0[:, k * T0 * D:(k + 1) * T0 * D].rearrange("p (t d) -> p t d", d=D) for k in range(2))
            member = in0[:, 2 * T0 * D:]
            h0 = sb0("h0", [P, T0, D])
            w1 = sb0("w1", [P, HID])
            ma = sb0("ma", [P, T0, G0, P])
            gt1 = sb0("gt1", [P, T0, G0 * P])
            w0 = sb0("w0", [P, 2 * G0 * E0])
            w10 = w0[:, 0:G0 * E0].rearrange("p (g e) -> p g e", e=E0)
            w20 = w0[:, G0 * E0:].rearrange("p (g c d) -> p g c d", c=2, d=D)
        adjH = sb("adjH", [P, 2 * NB * N], F32R)
        with ExitStack() as early:
            b0 = sb0("b0", [P, G0 * (E0 + D)])
            b10, b20 = b0[:, 0:G0 * E0], b0[:, G0 * E0:]
            h10 = sb0("h10", [P, 2, T0 * E0])
            gt2 = sb0("gt2", [P, 2, T0 * E0])
            o0 = sb0("o0", [P, 2, T0 * D])
            fus = sb0("fus", [P, G0])
            fmx = sb0("fmx", [P, 2])
            fex = sb0("fex", [P, G0])
            fsum = sb0("fsum", [P, 2])
            cw = sb0("cw", [P, G0])
            st0 = sb0("st0", [P, T0, 6])
            mv0 = sb0("mv0", [P, T0, 2])
            ve0 = sb0("ve0", [P, T0])
            rs0 = sb0("rs0", [P, T0])
            dg0 = sb0("dg0", [P, 4, T0 * G0])
            di0 = sb0("di0", [P, T0 * G0])
            wself = sb0("wself", [P, D])
            epsI = sb0("epsI", [P, P])
            b1r2 = sb0("b1r2", [2, HID])
            b1hi = sb0("b1hi", [2, HID], F32R)
            b1lo = sb0("b1lo", [2, HID])
        adjL = sb("adjL", [P, 2 * NB * N], F32R)

        l0_w2, l0_b = sem("l0_w2"), sem("l0_b")
        l0_in, l0_w, w_in, const_ready = sem("l0_in"), sem("l0_w"), sem("w_in"), sem("const_ready")
        s0_dve, s0_pool, s0_act = sem("layer0_dve"), sem("layer0_pool"), sem("layer0_act")
        s0_own = sem("layer0_dve_own")
        s0_pe, x0_stored = sem("layer0_pe"), sem("x0_stored")
        gt1_copied = sem("gt1_copied")
        c1_mm, g2_mm, out_mm = sem("c1_mm"), sem("g2_mm"), sem("out_mm")
        c1_scaled, c1_relu, g2_copied = sem("c1_scaled"), sem("c1_relu"), sem("g2_copied")
        out_scaled, out_weighted, x0_added = sem("out_scaled"), sem("out_weighted"), sem("x0_added")
        first_steps, first_pow, first_rstd = sem("first_steps"), sem("first_pow"), sem("first_rstd")
        first_relu, first_hi, first_lo = sem("first_relu"), sem("first_hi"), sem("first_lo")
        raw_in = [sem(f"raw_in_{s}") for s in range(RS)]
        xm_in, x0_in = sem("x_in"), sem("x_layer0_in")
        hi_ready, lo_ready = sem("hi_ready"), sem("lo_ready")
        summed = sem("summed")
        sc_kept = sem("scales_kept")
        rs_mm, deg_steps, deg_pow = sem("rs_mm"), sem("deg_steps"), sem("deg_pow")
        ln_steps = {k: sem(k + "_steps") for k in ln}
        pow_done = {k: sem(k + "_pow") for k in ln}
        ln_rstd = {k: sem(k + "_rstd") for k in ln}
        relu_done = {k: sem(k + "_relu") for k in ("ln1", "ln2a")}
        h3_done = [sem("h3_done_0"), sem("h3_done_1")]
        vH = {k: sem(f"v{k}_hi") for k in (1, 2, 3)}
        vL = {k: sem(f"v{k}_lo") for k in (1, 2, 3)}
        xb2 = sem("x_plus_b2")
        a1_mm, a2_mm = sem("a1_mm"), sem("a2_mm")
        a3_tile = sem("a3_tile")
        agg_hi, agg_lo = sem("agg_hi"), sem("agg_lo")
        nb_copied, o_copied = sem("nb_copied"), sem("o_copied")
        nb_copied2, o_copied2 = sem("nb_copied2"), sem("o_copied2")
        w1_mm, turn_mm, w2_mm = sem("w1_mm"), sem("turn_mm"), sem("w2_mm")
        squared, msq, rms, weighted = sem("squared"), sem("mean_square"), sem("rms"), sem("weighted")
        silu_done, sT_copied, x1_done = sem("silu_done"), sem("sT_copied"), sem("x1_done")
        xn_steps, v2_scaled = sem("xn_steps"), sem("v2_scaled")
        xnT_mm, xnT_copied, p1_mm, p1_copied, p2_mm = (sem(s) for s in ("xnT_mm", "xnT_copied", "p1_mm", "p1_copied", "p2_mm"))
        z_done, xz_done, sp_steps, x2_done = sem("z_done"), sem("x_relu_z"), sem("softplus_steps"), sem("x2_done")
        hT_mm, hT_copied, t3_mm, v3_steps = sem("hT_mm"), sem("hT_copied"), sem("t3_mm"), sem("v3_steps")
        oT_mm, o_scaled, x3_done = sem("oT_mm"), sem("o_scaled"), sem("x3_done")
        stored = [sem("stored_0"), sem("stored_1")]

        def xcols(graph, k0, k):
            return X[:, bass.ds((graph % XS) * N + k0 * D, k * D)]

        def tile_cols(graph, j, c0, c):
            return bass.ds(((graph + 1) % 2) * (NB * N) + j * N + c0, c)

        def blk(ap, k):
            return ap[:, k * D:(k + 1) * D]

        def by_block(ap):
            return ap.rearrange("p (k d) -> p k d", d=D)

        def over_blocks(ap, k=HB):
            return ap[:, :].unsqueeze(1).broadcast_to([P, k, D])

        block = ctx.enter_context(nc.Block())

        @block.sync
        def _(sp):
            def load(c):
                for g in range(2):
                    need(sp, stored[g], cnt(c - XS, 16, 16) if not isinstance(c, int) or c >= XS else 0)
                if isinstance(c, int) and c == 0:
                    load_x(c)
                    load_tiles(c, 0, 2)
                    sp.wait_ge(l0_w, 16)
                    load_tiles(c, 2, RS)
                    sp.dma_start(weights_in[:], t_in["weights"]).then_inc(w_in, 16)
                    sp.dma_start(w1[:], t_in["L1_gnn_W1"]).then_inc(w_in, 16)
                    sp.dma_start(wself[:], t_in["L2_gnn_W_self"]).then_inc(w_in, 16)
                    sp.dma_start(rows_in[:, :], t_in["rows"].partition_broadcast(P)).then_inc(w_in, 16)
                    sp.dma_start(b1r2[:, :], t_in["L1_gnn_b1"].partition_broadcast(2)).then_inc(w_in, 16)
                    load_tiles(c, RS, NB)
                    load_x(1)
                    sp.wait_ge(x0_added, G0)
                    sp.dma_start(x0_d.rearrange("t p d -> p t d"), xr).then_inc(x0_stored, 16)
                    sp.wait_ge(x0_stored, 16)
                elif isinstance(c, int) and c == 1:
                    sp.wait_ge(first_steps, 1)
                    load_x0(c)
                    load_tiles(c, 0, NB)
                else:
                    sp.wait_ge(x0_in, cnt(c - 1, 16, 16))
                    load_x(c)
                    load_x0(c)
                    load_tiles(c, 0, NB)

            def load_x(c):
                sp.dma_start(by_block(xcols(c, 0, NB)),
                             x_d[bass.ds(c, 1)].rearrange("a (k p) d -> p (a k) d", p=P)).then_inc(xm_in, 16)

            def load_x0(c):
                sp.wait_ge(xm_in, cnt(c, 16, 16))
                sp.dma_start(xcols(c, 0, 1)[0:N0, :],
                             x0_d.rearrange("t (b n) d -> (t b) n d", n=S0)[bass.ds(c, 1), 0:N0, :]
                             .rearrange("a n d -> (a n) d")).then_inc(x0_in, 16)

            def load_tiles(c, j0, j1):
                for j in range(j0, j1):
                    if j >= RS:
                        sp.wait_ge(lo_ready, cnt(c, NB, (j - RS) // 2 * 2 + 2))
                    elif j == 0 and (not isinstance(c, int) or c):
                        sp.wait_ge(lo_ready, cnt(c - 1, NB, NB))
                        sp.wait_ge(summed, cnt(c - 1, 2 * (NB - 1), 2 * (NB - 1)))
                    sp.dma_start(raw[:, j % RS, :],
                                 adjT_d[bass.ds(c, 1), j * P:(j + 1) * P, :].rearrange("a p n -> p (a n)")
                                 ).then_inc(raw_in[j % RS], 16)

            def store(p):
                for g in range(2):
                    sp.wait_ge(x3_done, cnt(p, 2, g + 1))
                    sp.dma_start(out[bass.ds(p, 1), g * HALF:(g + 1) * HALF, :].rearrange("a (k p) d -> p (a k) d", p=P),
                                 by_block(xcols(p, g * HB, HB))).then_inc(stored[g], 16)

            load(0)
            load(1)
            load(2)
            store(0)
            with sp.Fori(2, B - 1) as i:
                load(i + 1)
                store(i - 1)
            for p in range(B - 2, B):
                store(p)
            for g in range(2):
                sp.wait_ge(stored[g], 16 * B)

        @block.tensor
        def _(pe):
            mm = nc.tensor.matmul

            def layer0():
                pe.wait_ge(s0_dve, 1)
                for tt in range(T0):
                    last = mm(acc12[0][:, tt * G0:(tt + 1) * G0], adj0[:, tt, :], member, start=True, stop=True)
                last.then_inc(s0_pe, 1)
                pe.wait_ge(s0_act, 2)
                for tt in range(T0):
                    pe.wait_ge(s0_dve, 8 + tt)
                    m = ma[:, tt, :, :].rearrange("p g n -> p (g n)")
                    mm(acc3[tt][:, :], h0[:, tt, :], m[:, 0:HALF], start=True, stop=True)
                    mm(hid[tt][:, 0:P], h0[:, tt, :], m[:, HALF:], start=True, stop=True).then_inc(s0_pe, 1)
                pe.wait_ge(l0_w, 16)
                pe.wait_ge(gt1_copied, T0)
                for s in range(G0 + 2):
                    if s < G0:
                        need(pe, c1_scaled, s - 1)
                        for tt in range(T0):
                            last = mm(hid[s % 2][:, tt * E0:(tt + 1) * E0], gt1[:, tt, s * P:(s + 1) * P],
                                      w10[:, s, :], start=True, stop=True)
                        last.then_inc(c1_mm, 1)
                    if s == G0 - 1:
                        a1_start(1)
                    if 1 <= s <= G0:
                        r = s - 1
                        pe.wait_ge(c1_relu, r + 1)
                        need(pe, g2_copied, r)
                        for k in range(2 * T0):
                            last = mm(blk(turn, k), h10[:, r % 2, k * P:(k + 1) * P], ma[:, k // 2, r, :],
                                      start=True, stop=True)
                        last.then_inc(g2_mm, 1)
                    if s >= 2:
                        r = s - 2
                        if r == 0:
                            pe.wait_ge(l0_w2, 16)
                        pe.wait_ge(g2_copied, r + 1)
                        need(pe, out_scaled, r)
                        for k in range(2 * T0):
                            tt, c = k // 2, k % 2
                            last = mm(blk(mlp, tt), gt2[:, r % 2, k * P:(k + 1) * P], w20[:, r, c, :],
                                      start=(c == 0), stop=(c == 1))
                        last.then_inc(out_mm, 1)
                    if s >= G0:
                        a1_start(s - G0 + 2)

            def a1_start(j):
                pe.wait_ge(lo_ready, j + 1)
                a_tile(0, acc12, 1, v1H, v1L, j, False)

            def split_mm(dst, sH, sL, mH, mL, start, stop):
                mm(dst, sH, mH, start=start, stop=False)
                mm(dst, sH, mL, start=False, stop=False)
                return mm(dst, sL, mH, start=False, stop=stop)

            def a_tile(graph, acc, which, H, L, j, last_stop):
                first = 1 if which == 1 and isinstance(graph, int) and graph == 0 else 0
                if j == HB or j == first:
                    pe.wait_ge(vH[which], cnt(graph, 2, j // HB + 1))
                    pe.wait_ge(vL[which], cnt(graph, 2, j // HB + 1))
                for g in range(2):
                    last = split_mm(acc[g][:, :], blk(H, j), blk(L, j), adjH[:, tile_cols(graph, j, g * HALF, HALF)],
                                    adjL[:, tile_cols(graph, j, g * HALF, HALF)], j == first, last_stop and j == NB - 1)
                    if last_stop and j == NB - 1 and which == 2:
                        last.then_inc(a2_mm, 1)
                return last

            def phase_p(b, p):
                if p is not None:
                    for g in range(2):
                        pe.wait_ge(nb_copied if g == 0 else nb_copied2, cnt(p, 1, 1))
                        for k in range(HB):
                            last = mm(blk(hid[g], k), blk(colT, g * HB + k), wneigh[:, :], start=True, stop=True)
                        last.then_inc(p2_mm, 1)
                if b is not None:
                    order = [*range(4, NB), 0] if p is None else list(range(NB))
                    for j in order:
                        pe.wait_ge(lo_ready, cnt(b, NB, j + 1))
                        if j != order[-1]:
                            a_tile(b, acc12, 1, v1H, v1L, j, False)
                    if p is None:
                        pe.wait_ge(first_lo, 1)
                    j = order[-1]
                    for g in range(2):
                        cols = tile_cols(b, j, g * HALF, HALF)
                        split_mm(acc12[g][:, :], blk(v1H, j), blk(v1L, j), adjH[:, cols], adjL[:, cols], False, False)
                        if p is None and g == 0:
                            pe.wait_ge(const_ready, 6)
                        for k in range(HB):
                            n = g * HB + k
                            last = split_mm(blk(acc12[g], k), blk(v1H, n), blk(v1L, n), epsH[:, :], epsL[:, :],
                                            False, k == HB - 1)
                        last.then_inc(a1_mm, 1)

            def phase_q(b, p):
                for s in range(NB + 3):
                    if b is not None and s < NB:
                        if s % HB == 0:
                            pe.wait_ge(agg_lo, cnt(b, 2, s // HB + 1))
                        if s >= 2:
                            pe.wait_ge(weighted, cnt(b, NB, s - 1))
                            pe.wait_ge(squared, cnt(b, NB, s - 1))
                        elif p is not None:
                            pe.wait_ge(z_done, cnt(p, 2, s + 1))
                        split_mm(hid[s % 2][:, :], blk(aggH, s), blk(aggL, s), w1H[:, :], w1L[:, :], True, False)
                        mm(hid[s % 2][:, :], onesR[:, :], b1R[:, :], start=False, stop=True).then_inc(w1_mm, 1)
                    if p is not None and s in (1, 4):
                        layer3_turn(b, p, s // 4)
                    if b is not None and s in (1, 2):
                        if s == 1:
                            pe.wait_ge(summed, cnt(b, 2 * (NB - 1), 2 * (NB - 1)))
                        for k in range((s - 1) * HB, s * HB):
                            last = mm(acc3[1][:, k:k + 1], blk(rowsum, k), ones[:, :], start=True, stop=True)
                        last.then_inc(rs_mm, 1)
                    if p is not None and s in (3, 5):
                        layer3_transform(b, p, s // 2 - 1)
                    if p is not None and b is not None and s >= NB:
                        a3_tiles(p, s - NB, s - NB + 1)
                    if b is not None and 2 <= s <= NB + 1:
                        k = s - 2
                        pe.wait_ge(silu_done, cnt(b, NB, k + 1))
                        if k >= 1:
                            pe.wait_ge(sT_copied, cnt(b, NB, k))
                        elif p is not None:
                            pe.wait_ge(p1_copied, cnt(p, 2, 1))
                        for h in range(KH):
                            last = nc.tensor.transpose(blk(turn, h), blk(u[k % 2], h), ident[:, :])
                        last.then_inc(turn_mm, 1)
                    if b is not None and s >= 3:
                        k = s - 3
                        pe.wait_ge(sT_copied, cnt(b, NB, k + 1))
                        if k >= 1:
                            pe.wait_ge(x1_done, cnt(b, NB, k))
                        elif p is not None:
                            pe.wait_ge(p1_copied, cnt(p, 2, 2))
                        for h in range(KH):
                            last = mm(mlp[:, 0:D], blk(sT, h), blk(w2, h), start=(h == 0), stop=(h == KH - 1))
                        last.then_inc(w2_mm, 1)

            def a3_tiles(p, j0, j1):
                for j in range(j0, j1):
                    if j == 0:
                        pe.wait_ge(v3_steps, cnt(p, 4, 4))
                    a_tile(p, acc3, 3, v3H, v3L, j, True).then_inc(a3_tile, 1)

            def a3_by_halves(p):
                for g in range(2):
                    for j in range(NB):
                        if g == 0 and j % HB == 0:
                            pe.wait_ge(vH[3], cnt(p, 2, j // HB + 1))
                            pe.wait_ge(vL[3], cnt(p, 2, j // HB + 1))
                        cols = tile_cols(p, j, g * HALF, HALF)
                        last = split_mm(acc3[g][:, :], blk(v3H, j), blk(v3L, j), adjH[:, cols], adjL[:, cols],
                                        j == 0, j == NB - 1)
                        if g == 1 and j == 1:
                            output_turn(p, 0)
                    last.then_inc(a3_tile, 1)
                output_turn(p, 1)

            def output_turn(p, g):
                pe.wait_ge(o_copied if g == 0 else o_copied2, cnt(p, 1, 1))
                for k in range(HB):
                    last = nc.tensor.transpose(blk(acc3[g], k), blk(colT, g * HB + k), ident[:, :])
                last.then_inc(oT_mm, 1)

            def layer3_turn(b, p, g):
                pe.wait_ge(h3_done[g], cnt(p, 1, 1))
                if g == 0:
                    if b is None:
                        pe.wait_ge(o_scaled, cnt(p - 1, 2, 2))
                else:
                    pe.wait_ge(hT_copied, cnt(p, 2, g))
                for k in range(HB):
                    last = nc.tensor.transpose(blk(acc3[0], k), blk(t[g], k), ident[:, :])
                last.then_inc(hT_mm, 1)

            def layer3_transform(b, p, g):
                pe.wait_ge(hT_copied, cnt(p, 2, g + 1))
                if g == 1:
                    pe.wait_ge(v3_steps, cnt(p, 4, 1))
                elif b is not None:
                    pe.wait_ge(deg_steps, cnt(b, 4, 1))
                else:
                    pe.wait_ge(p1_copied, cnt(p, 2, 2))
                for k in range(HB):
                    last = mm(blk(acc3[1] if b is not None else mlp, k), blk(fT, k), w3[:, :], start=True, stop=True)
                last.then_inc(t3_mm, 1)

            def xn_turn(b, g):
                pe.wait_ge(xn_steps, cnt(b, 4, 2 * g + 2))
                pe.wait_ge(weighted, cnt(b, NB, NB - 1 + g))
                pe.wait_ge(squared, cnt(b, NB, NB - 1 + g))
                for k in range(HB):
                    last = nc.tensor.transpose(blk(hid[g], k), blk(xn, k), ident[:, :])
                last.then_inc(xnT_mm, 1)

            def xn_self(b, g):
                pe.wait_ge(xnT_copied, cnt(b, 2, g + 1))
                if g == 0:
                    pe.wait_ge(sT_copied, cnt(b, NB, NB))
                else:
                    pe.wait_ge(x1_done, cnt(b, NB, NB))
                for k in range(HB):
                    last = mm(blk(p1_bank[g], k), blk(fT, k), wsum[:, :], start=True, stop=True)
                last.then_inc(p1_mm, 1)

            def phase_r(b, p):
                if p is not None and b is None:
                    a3_by_halves(p)
                elif p is not None:
                    a3_tiles(p, 3, NB)
                if b is not None:
                    xn_turn(b, 0)
                for j in range(NB):
                    if b is not None:
                        a_tile(b, acc12, 2, v2H, v2L, j, True)
                        if j == 1:
                            xn_self(b, 0)
                    if b is not None and p is not None and j == 2:
                        for g in range(2):
                            output_turn(p, g)
                    if b is not None and j == NB - 3:
                        xn_turn(b, 1)
                if b is not None:
                    xn_self(b, 1)

            layer0()
            phase_p(0, None)
            phase_q(0, None)
            phase_r(0, None)
            with pe.Fori(1, B) as i:
                phase_p(i, i - 1)
                phase_q(i, i - 1)
                phase_r(i, i - 1)
            phase_p(None, B - 1)
            phase_q(None, B - 1)
            phase_r(None, B - 1)

        @block.scalar
        def _(act):
            a = nc.scalar.activation

            act.dma_start(in0[:], t_in["in0"]).then_inc(l0_in, 16)
            act.dma_start(ident[:, :], t_in["ident"]).then_inc(l0_in, 16)
            act.dma_start(fus[:, :], t_in["L0_gnn_fusion_w"].partition_broadcast(P)).then_inc(l0_in, 16)
            act.dma_start(w0[:, 0:G0 * E0], t_in["w0"][:, 0:G0 * E0]).then_inc(l0_w, 16)
            act.dma_start(b0[:, :], t_in["b0"].partition_broadcast(P)).then_inc(l0_b, 16)
            act.dma_start(w0[:, G0 * E0:], t_in["w0"][:, G0 * E0:]).then_inc(l0_w2, 16)

            def split_hi(c, j):
                act.wait_ge(raw_in[j % RS], cnt(c, 16 * (NB // RS), 16 * (j // RS + 1)))
                if j < NB - 2 and (not isinstance(c, int) or c >= 2):
                    act.wait_ge(a3_tile, cnt(c - 2, NB, j + 1))
                if j == 0 and (not isinstance(c, int) or c >= 1):
                    act.wait_ge(deg_steps, cnt(c - 1, 4, 3))
                a(adjH[:, tile_cols(c, j, 0, N)], raw[:, j % RS, :], ACT.Copy,
                  accum_out=deg[:, NB + j:NB + j + 1]).then_inc(hi_ready, 1)

            def layer0():
                split_hi(0, 0)
                act.wait_ge(s0_dve, 4)
                a(fex[:, :], fus[:, :], ACT.Exp, bias=fmx[:, 1:2], accum_out=fsum[:, 0:1]).then_inc(s0_act, 1)
                split_hi(0, 1)
                act.wait_ge(s0_dve, 7)
                a(h0[:].rearrange("p t d -> p (t d)"), h0[:].rearrange("p t d -> p (t d)"), ACT.Relu).then_inc(s0_act, 1)
                for tt in range(T0):
                    act.wait_ge(s0_pe, 2 + tt)
                    a(gt1[:, tt, 0:HALF], acc3[tt][:, :], ACT.Copy)
                    a(gt1[:, tt, HALF:], hid[tt][:, 0:P], ACT.Copy).then_inc(gt1_copied, 1)
                    split_hi(0, 2 + tt)
                for s in range(G0 + 2):
                    if s < G0:
                        act.wait_ge(c1_scaled, s + 1)
                        a(h10[:, s % 2, :], h10[:, s % 2, :], ACT.Relu).then_inc(c1_relu, 1)
                    if 1 <= s <= G0:
                        r = s - 1
                        act.wait_ge(g2_mm, r + 1)
                        need(act, out_mm, r - 1)
                        a(gt2[:, r % 2, :], turn[:, :], ACT.Copy).then_inc(g2_copied, 1)
                    if s >= 2:
                        r = s - 2
                        act.wait_ge(out_scaled, r + 1)
                        a(o0[:, 1, :], o0[:, 0, :], ACT.Relu, scale=cw[:, r:r + 1]).then_inc(out_weighted, 1)
                    if s < 2:
                        relu("ln1", 0, s)
                        v_hi(1, v1H, 0, s, relu_done["ln1"], s + 1)
                    if 2 <= s < 2 + NB - RS:
                        split_hi(0, RS + s - 2)

            def first_block():
                act.wait_ge(first_rstd, 1)
                a(blk(t1[0], 0), xcols(0, 0, 1), ACT.Relu, scale=rstd["ln1"][0][:, 0:1],
                  bias=shift["ln1"][0][:, 0:1]).then_inc(first_relu, 1)
                act.wait_ge(first_relu, 1)
                a(v1H[:, 0:D], blk(t1[0], 0), ACT.Copy).then_inc(first_hi, 1)

            def relu(kind, graph, g):
                act.wait_ge(ln_rstd[kind], cnt(graph, 2, g + 1))
                dst = t1[g] if kind == "ln1" else t[g]
                for k in range(HB):
                    last = a(blk(dst, k), xcols(graph, g * HB + k, 1), ACT.Relu, scale=rstd[kind][g][:, k:k + 1],
                             bias=shift[kind][g][:, k:k + 1])
                last.then_inc(relu_done[kind], 1)

            def v_hi(which, H, graph, g, ready, value):
                act.wait_ge(ready, value)
                a(H[:, g * HALF:(g + 1) * HALF], (t1 if which == 1 else t)[g][:, :], ACT.Copy).then_inc(vH[which], 1)

            def phase_p(b, p):
                if p is not None:
                    act.wait_ge(nb_copied2, cnt(p, 1, 1))
                    for g in range(2):
                        act.wait_ge(p1_mm, cnt(p, 2, g + 1))
                        a(z[g][:, :], p1_bank[g][:, :], ACT.Copy).then_inc(p1_copied, 1)
                    a(warm[:, :], ones[:, :], ACT.Exp)
                    if b is not None:
                        for j in range(NB - 2, NB):
                            split_hi(b, j)
                    for g in range(2):
                        act.wait_ge(z_done, cnt(p, 2, g + 1))
                        a(t[g][:, :], z[g][:, :], ACT.Abs).then_inc(sp_steps, 1)
                    for g in range(2):
                        act.wait_ge(sp_steps, cnt(p, 6, 1 + g))
                        a(t[g][:, :], t[g][:, :], ACT.Exp, scale=-1.0).then_inc(sp_steps, 1)
                    for g in range(2):
                        act.wait_ge(sp_steps, cnt(p, 6, 3 + g))
                        a(t[g][:, :], t[g][:, :], ACT.Ln, bias=1.0).then_inc(sp_steps, 1)
                if b is not None:
                    a(warm[:, :], ones[:, :], ACT.Silu)
                    agg_hi_part(b, 0)
                if p is not None:
                    act.wait_ge(ln_steps["ln3"], cnt(p, 6, 3))
                    for k in range(HB):
                        last = a(blk(t[0], k), xcols(p, k, 1), ACT.Relu, bias=negmean["ln3"][0][:, k:k + 1])
                    last.then_inc(h3_done[0], 1)

            def agg_hi_part(b, g):
                act.wait_ge(a1_mm, cnt(b, 2, g + 1))
                a(aggH[:, g * HALF:(g + 1) * HALF], acc12[g][:, :], ACT.Copy).then_inc(agg_hi, 1)

            def phase_q(b, p, c):
                for s in range(NB + 2):
                    if b is not None and s < NB:
                        act.wait_ge(w1_mm, cnt(b, NB, s + 1))
                        if s >= 2:
                            act.wait_ge(msq, cnt(b, NB, s - 1))
                        if not isinstance(b, int) or b or s:
                            act.wait_ge(squared, cnt(b, NB, s))
                        a(junk[:, :], hid[s % 2][:, :], ACT.Square, scale=HID ** -0.5,
                          accum_out=ss[:, s % 2:s % 2 + 1]).then_inc(squared, 1)
                        if s == 1:
                            agg_hi_part(b, 1)
                    if p is not None and s in (1, 4):
                        turn3_copy(p, s // 4)
                    if b is not None and 1 <= s <= NB:
                        k = s - 1
                        act.wait_ge(rms, cnt(b, NB, k + 1))
                        act.wait_ge(weighted, cnt(b, NB, k + 1))
                        a(u[k % 2][:, :], u[k % 2][:, :], ACT.Silu, scale=rrms[:, k % 2:k % 2 + 1]).then_inc(silu_done, 1)
                    if b is not None and 2 <= s <= NB + 1:
                        k = s - 2
                        act.wait_ge(turn_mm, cnt(b, NB, k + 1))
                        if k >= 1:
                            act.wait_ge(w2_mm, cnt(b, NB, k))
                        a(sT[:, :], turn[:, :], ACT.Copy).then_inc(sT_copied, 1)
                    if b is not None and s == NB:
                        relu("ln2a", b, 0)

            def turn3_copy(p, g):
                act.wait_ge(hT_mm, cnt(p, 2, g + 1))
                if g == 1:
                    act.wait_ge(t3_mm, cnt(p, 2, 1))
                else:
                    act.wait_ge(p1_mm, cnt(p, 2, 2))
                a(fT[:, :], acc3[0][:, :], ACT.Copy).then_inc(hT_copied, 1)

            def phase_r(b, p, c):
                if c is not None:
                    for j in range(3):
                        split_hi(c, j)
                if b is not None:
                    v_hi(2, v2H, b, 0, v2_scaled, cnt(b, 2, 1))
                if c is not None:
                    split_hi(c, 3)
                if b is not None:
                    relu("ln2a", b, 1)
                if p is not None:
                    act.wait_ge(a3_tile, cnt(p, NB, NB if b is not None else 1))
                    a(colT[:, 0:HALF], acc3[0][:, :], ACT.Copy).then_inc(o_copied, 1)
                if b is not None:
                    act.wait_ge(xnT_mm, cnt(b, 2, 1))
                    if p is not None:
                        act.wait_ge(t3_mm, cnt(p, 2, 2))
                    a(fT[:, :], hid[0][:, :], ACT.Copy).then_inc(xnT_copied, 1)
                if c is not None:
                    for g in range(2):
                        relu("ln1", c, g)
                if b is not None:
                    v_hi(2, v2H, b, 1, v2_scaled, cnt(b, 2, 2))
                if c is not None:
                    for j in range(4, NB - 2):
                        split_hi(c, j)
                    v_hi(1, v1H, c, 0, relu_done["ln1"], cnt(c, 2, 1))
                if b is not None:
                    act.wait_ge(xnT_mm, cnt(b, 2, 2))
                    act.wait_ge(p1_mm, cnt(b, 2, 1))
                    a(fT[:, :], hid[1][:, :], ACT.Copy).then_inc(xnT_copied, 1)
                if c is not None:
                    v_hi(1, v1H, c, 1, relu_done["ln1"], cnt(c, 2, 2))
                if b is not None:
                    act.wait_ge(a2_mm, cnt(b, 2, 1))
                    if p is not None:
                        act.wait_ge(oT_mm, cnt(p, 2, 2))
                    a(colT[:, 0:HALF], acc12[0][:, :], ACT.Copy).then_inc(nb_copied, 1)

            layer0()
            first_block()
            phase_p(0, None)
            phase_q(0, None, 1)
            phase_r(0, None, 1)
            with act.Fori(1, B - 1) as i:
                phase_p(i, i - 1)
                phase_q(i, i - 1, i + 1)
                phase_r(i, i - 1, i + 1)
            phase_p(B - 1, B - 2)
            phase_q(B - 1, B - 2, None)
            phase_r(B - 1, B - 2, None)
            phase_p(None, B - 1)
            phase_q(None, B - 1, None)
            phase_r(None, B - 1, None)

        @block.vector
        def _(dve):
            v = nc.vector

            def setup():
                v.memset(ones[:, :], 1.0)
                v.memset(rms_eps[:, :], 1e-6)
                v.memset(power[:, :], -0.5).then_inc(const_ready, 1)

            def layer0():
                dve.wait_ge(l0_in, 16 * 3)
                i2 = ident[:, :].unsqueeze(1).broadcast_to([P, T0, P])
                v.tensor_tensor(adj0, adj0, i2, ALU.add).then_inc(s0_dve, 1)
                for tt in range(T0):
                    last = v.bn_stats(st0[:, tt, :], xr[:, tt, :])
                last.then_inc(s0_dve, 1)
                v.tensor_reduce(fmx[:, 0:1], fus[:, :], AX.X, ALU.max).then_inc(s0_dve, 1)
                dve.wait_ge(s0_dve, 3)
                for tt in range(T0):
                    v.bn_aggr(mv0[:, tt, :], st0[:, tt, :])
                v.tensor_scalar(fmx[:, 1:2], fmx[:, 0:1], -1.0, None, ALU.mult).then_inc(s0_dve, 1)
                dve.wait_ge(s0_dve, 4)
                v.tensor_scalar(ve0[:, :], mv0[:, :, 1], 1e-5, None, ALU.add).then_inc(s0_dve, 1)
                dve.wait_ge(s0_pe, 1)
                v.tensor_tensor(dg0[:, 0, :].rearrange("p (t g) -> p t g", g=G0),
                                acc12[0][:, 0:T0 * G0].rearrange("p (t g) -> p t g", g=G0),
                                member.unsqueeze(1).broadcast_to([P, T0, G0]), ALU.mult).then_inc(s0_own, 1)
                dve.wait_ge(s0_own, 1)
                v.tensor_scalar(dg0[:, 1, :], dg0[:, 0, :], 0.0, None, ALU.not_equal)
                v.tensor_scalar(dg0[:, 2, :], dg0[:, 0, :], 0.0, None, ALU.is_equal).then_inc(s0_own, 1)
                dve.wait_ge(s0_own, 2)
                v.tensor_tensor(dg0[:, 2, :], dg0[:, 2, :], dg0[:, 0, :], ALU.add).then_inc(s0_dve, 1)
                dve.wait_ge(s0_pool, 1)
                for tt in range(T0):
                    last = v.tensor_scalar(h0[:, tt, :], xr[:, tt, :], mv0[:, tt, 0:1], rs0[:, tt:tt + 1],
                                           ALU.subtract, ALU.mult)
                last.then_inc(s0_dve, 1)
                dve.wait_ge(s0_pool, 2)
                v.tensor_tensor(di0[:, :], dg0[:, 3, :], dg0[:, 1, :], ALU.mult).then_inc(s0_own, 1)
                dve.wait_ge(s0_own, 3)
                for tt in range(T0):
                    v.tensor_tensor(ma[:, tt, :, :], adj0[:, tt, :].unsqueeze(1).broadcast_to([P, G0, P]),
                                    di0[:, tt * G0:(tt + 1) * G0].unsqueeze(2).broadcast_to([P, G0, P]), ALU.mult
                                    ).then_inc(s0_dve, 1)
                dve.wait_ge(s0_act, 1)
                v.reciprocal(fsum[:, 1:2], fsum[:, 0:1]).then_inc(s0_own, 1)
                dve.wait_ge(s0_own, 4)
                v.scalar_tensor_tensor(cw[:, :], fex[:, :], fsum[:, 1:2], member, ALU.mult, ALU.mult
                                       ).then_inc(s0_dve, 1)
                dve.wait_ge(xm_in, 16)
                for g in range(2):
                    stats("ln1", 0, g, xsrc(0, g))
                split_lo(0, 0)
                dve.wait_ge(l0_b, 16)
                for s in range(G0 + 2):
                    if s < G0:
                        dve.wait_ge(c1_mm, s + 1)
                        need(dve, g2_mm, s - 1)
                        for tt in range(T0):
                            q = tt * G0 + s
                            cols = slice(tt * E0, (tt + 1) * E0)
                            last = v.scalar_tensor_tensor(h10[:, s % 2, cols], hid[s % 2][:, cols], di0[:, q:q + 1],
                                                          b10[:, s * E0:(s + 1) * E0], ALU.mult, ALU.add)
                        last.then_inc(c1_scaled, 1)
                    if s >= 2:
                        r = s - 2
                        dve.wait_ge(out_mm, r + 1)
                        need(dve, out_weighted, r)
                        for tt in range(T0):
                            q = tt * G0 + r
                            last = v.scalar_tensor_tensor(o0[:, 0, tt * D:(tt + 1) * D], blk(mlp, tt), di0[:, q:q + 1],
                                                          b20[:, r * D:(r + 1) * D], ALU.mult, ALU.add)
                        last.then_inc(out_scaled, 1)
                    if s < RS - 1:
                        split_lo(0, s + 1)
                    if s in (3, 4):
                        v_lo(1, v1H, v1L, 0, s - 3)
                    if s >= 5:
                        weights(s - 3)
                    if s >= 2:
                        dve.wait_ge(out_weighted, r + 1)
                        v.tensor_tensor(in0[:, 0:T0 * D], in0[:, 0:T0 * D], o0[:, 1, :], ALU.add).then_inc(x0_added, 1)
                        if 3 <= s < G0 + 1:
                            split_lo(0, RS + s - 3)
                        dve.wait_ge(x0_added, r + 1)

            def first_block():
                v.tensor_copy(xcols(0, 0, 1)[0:N0, :], xr[0:N0, 0, :]).then_inc(x0_in, 16)
                dve.wait_ge(x0_in, 16)
                v.bn_stats(stat6[:, 0, :], xcols(0, 0, 1)).then_inc(first_steps, 1)
                dve.wait_ge(first_steps, 1)
                v.bn_aggr(mv["ln1"][0][:, 0, :], stat6[:, 0, :]).then_inc(first_steps, 1)
                dve.wait_ge(first_steps, 2)
                v.tensor_scalar(negmean["ln1"][0][:, 0:1], mv["ln1"][0][:, 0, 0:1], -1.0, None, ALU.mult)
                v.tensor_scalar(veps["ln1"][0][:, 0:1], mv["ln1"][0][:, 0, 1:2], 1e-5, None, ALU.add
                                ).then_inc(first_steps, 1)
                split_lo(0, NB - 1)
                weights(4)
                weights(5)
                dve.wait_ge(first_hi, 1)
                v.tensor_tensor(v1L[:, 0:D], blk(t1[0], 0), v1H[:, 0:D].bitcast(F32), ALU.subtract).then_inc(first_lo, 1)

            def weights(step):
                if step == 2:
                    dve.wait_ge(w_in, 16 * 5)
                    v.tensor_tensor(wsum[:, :], wself[:, :], wneigh, ALU.add)
                    v.tensor_copy(w1H[:, :], w1[:, :])
                    v.tensor_scalar(epsI[:, :], ident[:, :], eps[:, 0:1], None, ALU.mult)
                    v.tensor_copy(b1hi[:, :], b1r2[:, :])
                    v.tensor_copy(onesR[:, :], ones[0:2, :].broadcast_to([2, P])).then_inc(const_ready, 1)
                    return
                dve.wait_ge(const_ready, step - 1)
                if step == 3:
                    v.tensor_copy(epsH[:, :], epsI[:, :])
                    v.tensor_tensor(w1L[:, :], w1[:, :], w1H[:, :].bitcast(F32), ALU.subtract).then_inc(const_ready, 1)
                elif step == 4:
                    v.tensor_tensor(b1lo[:, :], b1r2[:, :], b1hi[:, :].bitcast(F32), ALU.subtract)
                    v.tensor_tensor(epsL[:, :], epsI[:, :], epsH[:, :].bitcast(F32), ALU.subtract).then_inc(const_ready, 1)
                elif step == 5:
                    v.tensor_scalar(b1lo[:, :], b1lo[:, :], ident[0:2, 1:2], None, ALU.mult).then_inc(const_ready, 1)
                elif step == 6:
                    v.scalar_tensor_tensor(b1R[:, :], b1hi[:, :].bitcast(F32), ident[0:2, 0:1], b1lo[:, :],
                                           ALU.mult, ALU.add).then_inc(const_ready, 1)

            def split_lo(c, j):
                dve.wait_ge(hi_ready, cnt(c, NB, j + 1))
                if j < RS and j % 2:
                    dve.wait_ge(summed, cnt(c, 2 * (NB - 1), 2 * j))
                cols = tile_cols(c, j, 0, N)
                v.tensor_tensor(adjL[:, cols], raw[:, j % RS, :], adjH[:, cols].bitcast(F32), ALU.subtract
                                ).then_inc(lo_ready, 1)

            def stats(kind, graph, g, source):
                v.tensor_copy(tick[:, 0:1], power[:, 0:1])
                for k in range(HB):
                    last = v.bn_stats(stat6[:, k, :], source(k))
                last.then_inc(ln_steps[kind], 1)
                stats_end(kind, graph, g, stat6)

            def stats_end(kind, graph, g, parts):
                steps = ln_steps[kind]
                dve.wait_ge(steps, cnt(graph, 6, 3 * g + 1))
                v.tensor_copy(tick[:, 1:2], power[:, 0:1])
                for k in range(HB):
                    last = v.bn_aggr(mv[kind][g][:, k, :], parts[:, k, :])
                last.then_inc(steps, 1)
                dve.wait_ge(steps, cnt(graph, 6, 3 * g + 2))
                v.tensor_scalar(negmean[kind][g][:, :], mv[kind][g][:, :, 0], -1.0, None, ALU.mult)
                v.tensor_scalar(veps[kind][g][:, :], mv[kind][g][:, :, 1], 1e-5, None, ALU.add).then_inc(steps, 1)

            def v_lo(which, H, L, graph, g):
                dve.wait_ge(vH[which], cnt(graph, 2, g + 1))
                cols = slice(g * HALF, (g + 1) * HALF)
                v.tensor_tensor(L[:, cols], (t1 if which == 1 else t)[g][:, :], H[:, cols].bitcast(F32), ALU.subtract).then_inc(vL[which], 1)

            def xsrc(graph, g):
                return lambda k: xcols(graph, g * HB + k, 1)

            def tsrc(g):
                return lambda k: blk(t[g], k)

            def degrees(b):
                dve.wait_ge(deg_steps, cnt(b, 4, 1))
                dve.wait_ge(hi_ready, cnt(b, NB, NB))
                v.tensor_scalar(dz[:, :], deg[:, :], 0.0, None, ALU.is_equal)
                v.tensor_scalar(dnz[:, 0:NB], deg[:, 0:NB], 0.0, None, ALU.not_equal)
                v.tensor_scalar(dnz[:, NB:], deg[:, NB:], 0.0, -1.0, ALU.not_equal, ALU.mult).then_inc(deg_steps, 1)
                dve.wait_ge(deg_steps, cnt(b, 4, 2))
                v.tensor_tensor(dsafe[:, :], deg[:, :], dz[:, :], ALU.add).then_inc(deg_steps, 1)

            def agg_lo_part(b, g):
                dve.wait_ge(agg_hi, cnt(b, 2, g + 1))
                cols = slice(g * HALF, (g + 1) * HALF)
                v.tensor_tensor(aggL[:, cols], acc12[g][:, :], aggH[:, cols].bitcast(F32), ALU.subtract).then_inc(agg_lo, 1)

            def degrees_end(b):
                dve.wait_ge(deg_pow, cnt(b, 1, 1))
                v.tensor_tensor(sc_b[:, :], dpow[:, :], dnz[:, :], ALU.mult).then_inc(deg_steps, 1)

            def phase_p(b, p, c):
                if p is not None:
                    v.tensor_copy(sc_p[:, :], sc_b[:, :]).then_inc(sc_kept, 1)
                    dve.wait_ge(sc_kept, cnt(p, 1, 1))
                    for g in range(2):
                        dve.wait_ge(p1_copied, cnt(p, 2, g + 1))
                        dve.wait_ge(p2_mm, cnt(p, 2, g + 1))
                        for k in range(HB):
                            n = g * HB + k
                            last = v.scalar_tensor_tensor(blk(z[g], k), blk(hid[g], k), sc_p[:, NB + n:NB + n + 1],
                                                          blk(z[g], k), ALU.mult, ALU.add)
                        last.then_inc(z_done, 1)
                    for g in range(2):
                        dve.wait_ge(z_done, cnt(p, 2, g + 1))
                        v.scalar_tensor_tensor(xcols(p, g * HB, HB), z[g][:, :], 0.0, xcols(p, g * HB, HB),
                                               ALU.max, ALU.add).then_inc(xz_done, 1)
                    if b is not None:
                        for j in range(NB - 2, NB):
                            split_lo(b, j)
                if c is not None:
                    stats_1(c, 0)
                if p is not None:
                    for g in range(2):
                        if b is not None and g == 1:
                            agg_lo_part(b, 0)
                        dve.wait_ge(xz_done, cnt(p, 2, g + 1))
                        dve.wait_ge(sp_steps, cnt(p, 6, 5 + g))
                        v.tensor_tensor(xcols(p, g * HB, HB), xcols(p, g * HB, HB), t[g][:, :], ALU.add
                                        ).then_inc(x2_done, 1)
                        dve.wait_ge(x2_done, cnt(p, 2, g + 1))
                        stats("ln3", p, g, xsrc(p, g))
                elif b is not None:
                    agg_lo_part(b, 0)

            def phase_q(b, p, c):
                for s in range(NB + 3):
                    if b is not None and s == 2:
                        dve.wait_ge(rs_mm, cnt(b, 2, 2))
                        v.tensor_copy(deg[:, 0:NB], acc3[1][:, 0:NB]).then_inc(deg_steps, 1)
                    if b is not None and s < NB:
                        dve.wait_ge(w1_mm, cnt(b, NB, s + 1))
                        if s >= 2:
                            dve.wait_ge(turn_mm, cnt(b, NB, s - 1))
                        dve.wait_ge(squared, cnt(b, NB, s + 1))
                        v.tensor_tensor(u[s % 2][:, :], hid[s % 2][:, :], wrms[:, :], ALU.mult).then_inc(weighted, 1)
                        if s == 1:
                            agg_lo_part(b, 1)
                    if b is not None and s == 2:
                        degrees(b)
                    if b is not None and s >= 3:
                        k = s - 3
                        dve.wait_ge(w2_mm, cnt(b, NB, k + 1))
                        if k == 0:
                            dve.wait_ge(xb2, cnt(b, 1, 1))
                        v.tensor_tensor(xcols(b, k, 1), xcols(b, k, 1), mlp[:, 0:D], ALU.add).then_inc(x1_done, 1)
                    if p is not None and s == 2:
                        for k in range(HB):
                            last = v.tensor_scalar(blk(t[1], k), xcols(p, HB + k, 1), mv["ln3"][1][:, k, 0:1], 0.0,
                                                   ALU.subtract, ALU.max)
                        last.then_inc(h3_done[1], 1)
                    if p is not None and s in (3, 5):
                        g = s // 2 - 1
                        dve.wait_ge(pow_done["ln3"], cnt(p, 2, g + 1))
                        dve.wait_ge(t3_mm, cnt(p, 2, g + 1))
                        for k in range(HB):
                            bank3 = acc3[1] if b is not None else mlp
                            last = v.scalar_tensor_tensor(blk(t[g], k), blk(bank3, k), rstd["ln3"][g][:, k:k + 1],
                                                          b3bc, ALU.mult, ALU.add)
                        last.then_inc(v3_steps, 1)
                        dve.wait_ge(v3_steps, cnt(p, 4, 2 * g + 1))
                        for k in range(HB):
                            n = g * HB + k
                            last = v.tensor_scalar(blk(t[g], k), blk(t[g], k), sc_p[:, n:n + 1], None, ALU.mult)
                        last.then_inc(v3_steps, 1)
                    if p is not None and s in (4, 6):
                        g = s // 2 - 2
                        dve.wait_ge(v3_steps, cnt(p, 4, 2 * g + 2))
                        v.tensor_copy(v3H[:, g * HALF:(g + 1) * HALF], t[g][:, :]).then_inc(vH[3], 1)
                        v_lo(3, v3H, v3L, p, s // 2 - 2)
                    if b is not None and s >= HB:
                        x1_stats(b, s - HB)
                    if c is not None and s == NB:
                        stats_1(c, 1)
                    if b is not None and s == NB + 1:
                        xn_norm(b, 0)

            def x1_stats(b, k):
                dve.wait_ge(x1_done, cnt(b, NB, k + 1))
                v.tensor_copy(tick[:, 2 + k:3 + k], power[:, 0:1])
                last = v.bn_stats(stat6_x1[:, k % HB, :], xcols(b, k, 1))
                if k % HB == HB - 1:
                    last.then_inc(ln_steps["ln2a"], 1)
                    stats_end("ln2a", b, k // HB, stat6_x1)

            def xn_norm(b, g):
                dve.wait_ge(relu_done["ln2a"], cnt(b, 2, g + 1))
                stats("ln2b", b, g, tsrc(g))
                for k in range(HB):
                    last = v.scalar_tensor_tensor(blk(t[g], k), blk(t[g], k), mv["ln2b"][g][:, k, 0:1], gam[:, :],
                                                  ALU.subtract, ALU.mult)
                last.then_inc(xn_steps, 1)

            def xn_end(b, g):
                dve.wait_ge(pow_done["ln2b"], cnt(b, 2, g + 1))
                dve.wait_ge(xn_steps, cnt(b, 4, 2 * g + 1))
                if g == 1:
                    dve.wait_ge(xnT_mm, cnt(b, 2, 1))
                    dve.wait_ge(v2_scaled, cnt(b, 2, 1))
                for k in range(HB):
                    last = v.scalar_tensor_tensor(blk(xn, k), blk(t[g], k), rstd["ln2b"][g][:, k:k + 1], bet[:, :],
                                                  ALU.mult, ALU.add)
                last.then_inc(xn_steps, 1)

            def xn_scale(b, g):
                dve.wait_ge(xn_steps, cnt(b, 4, 2 * g + 2))
                for k in range(HB):
                    n = g * HB + k
                    last = v.tensor_scalar(blk(t[g], k), blk(xn, k), sc_b[:, n:n + 1], None, ALU.mult)
                last.then_inc(v2_scaled, 1)

            def output(b, p, g):
                dve.wait_ge(oT_mm, cnt(p, 2, g + 1))
                if b is not None:
                    dve.wait_ge(turn_mm, cnt(b, NB, NB))
                s_in = sc_p[:, g * HB:(g + 1) * HB].unsqueeze(2).broadcast_to([P, HB, D])
                v.scalar_tensor_tensor(by_block(z[g][:, :]), by_block(acc3[g][:, :]), 0.0, s_in,
                                       ALU.max, ALU.mult).then_inc(o_scaled, 1)
                dve.wait_ge(o_scaled, cnt(p, 2, g + 1))
                v.tensor_tensor(xcols(p, g * HB, HB), xcols(p, g * HB, HB), z[g][:, :], ALU.add
                                ).then_inc(x3_done, 1)

            def phase_r(b, p, c):
                if b is not None:
                    degrees_end(b)
                    xn_end(b, 0)
                    xn_scale(b, 0)
                    x1_stats(b, NB - 1)
                if b is not None:
                    v_lo(2, v2H, v2L, b, 0)
                if c is not None:
                    split_lo(c, 0)
                    split_lo(c, 1)
                if b is None:
                    output(b, p, 0)
                if p is not None:
                    dve.wait_ge(a3_tile, cnt(p, NB, NB if b is not None else 2))
                    v.tensor_copy(colT[:, HALF:], acc3[1][:, :]).then_inc(o_copied2, 1)
                if b is not None:
                    xn_norm(b, 1)
                if b is not None:
                    xn_end(b, 1)
                    xn_scale(b, 1)
                if b is not None:
                    v_lo(2, v2H, v2L, b, 1)
                if c is not None:
                    split_lo(c, 2)
                    split_lo(c, 3)
                if p is not None and b is not None:
                    output(b, p, 0)
                if c is not None:
                    split_lo(c, 4)
                if p is not None:
                    output(b, p, 1)
                if c is not None:
                    v_lo(1, v1H, v1L, c, 0)
                if b is not None:
                    dve.wait_ge(a2_mm, cnt(b, 2, 2))
                    if p is not None:
                        dve.wait_ge(oT_mm, cnt(p, 2, 2))
                    v.tensor_copy(colT[:, HALF:], acc12[1][:, :]).then_inc(nb_copied2, 1)
                if c is not None:
                    v_lo(1, v1H, v1L, c, 1)
                    split_lo(c, 5)

            def stats_1(c, g):
                if g == 0:
                    dve.wait_ge(x0_in, cnt(c, 16, 16))
                stats("ln1", c, g, xsrc(c, g))

            setup()
            layer0()
            first_block()
            weights(6)
            phase_p(0, None, 1)
            phase_q(0, None, 1)
            phase_r(0, None, 1)
            with dve.Fori(1, B - 1) as i:
                phase_p(i, i - 1, i + 1)
                phase_q(i, i - 1, i + 1)
                phase_r(i, i - 1, i + 1)
            phase_p(B - 1, B - 2, None)
            phase_q(B - 1, B - 2, None)
            phase_r(B - 1, B - 2, None)
            phase_p(None, B - 1, None)
            phase_q(None, B - 1, None)
            phase_r(None, B - 1, None)

        @block.gpsimd
        def _(pool):
            gp = nc.gpsimd

            def pw(dst, src, n):
                return gp.tensor_tensor(dst, src, power[:, 0:n], ALU.pow)

            def add_rows(c, j):
                for h in range(2):
                    add_half(c, j, h)

            def add_half(c, j, h):
                cols = slice(h * HALF, (h + 1) * HALF)
                if h == 0:
                    pool.wait_ge(raw_in[j % RS], cnt(c, 16 * (NB // RS), 16 * (j // RS + 1)))
                if j == 1:
                    if h == 0:
                        pool.wait_ge(raw_in[0], cnt(c, 16 * (NB // RS), 16))
                        if not isinstance(c, int) or c >= 1:
                            pool.wait_ge(rs_mm, cnt(c - 1, 2, 2))
                    first = raw[:, 0, cols]
                else:
                    pool.wait_ge(summed, cnt(c, 2 * (NB - 1), 2 * (j - 2) + h + 1))
                    first = rowsum[:, cols]
                gp.tensor_tensor(rowsum[:, cols], first, raw[:, j % RS, cols], ALU.add).then_inc(summed, 1)

            def rstd_of(kind, graph, g):
                pool.wait_ge(ln_steps[kind], cnt(graph, 6, 3 * g + 3))
                pw(rstd[kind][g][:, :], veps[kind][g][:, :], HB).then_inc(pow_done[kind], 1)
                if kind in ("ln2b", "ln3"):
                    return
                pool.wait_ge(pow_done[kind], cnt(graph, 2, g + 1))
                gp.tensor_tensor(shift[kind][g][:, :], negmean[kind][g][:, :], rstd[kind][g][:, :], ALU.mult
                                 ).then_inc(ln_rstd[kind], 1)

            def phase_p(b, p, c):
                if b is not None and p is not None:
                    for j in range(NB - 2, NB):
                        add_rows(b, j)
                if c is not None:
                    rstd_of("ln1", c, 0)
                if p is not None:
                    rstd_of("ln3", p, 0)
                    if b is None:
                        rstd_of("ln3", p, 1)

            def phase_q(b, p, c):
                for s in range(NB):
                    if b is not None:
                        pool.wait_ge(squared, cnt(b, NB, s + 1))
                        if s >= 2:
                            pool.wait_ge(silu_done, cnt(b, NB, s - 1))
                        e = s % 2
                        gp.tensor_tensor(sse[:, e:e + 1], ss[:, e:e + 1], rms_eps[:, :], ALU.add).then_inc(msq, 1)
                        pool.wait_ge(msq, cnt(b, NB, s + 1))
                        pw(rrms[:, e:e + 1], sse[:, e:e + 1], 1).then_inc(rms, 1)
                    if b is not None and p is not None and s == 0:
                        rstd_of("ln3", p, 1)
                    if c is not None and 2 <= s:
                        add_half(c, s // 2, s % 2)
                if b is not None:
                    rstd_of("ln2a", b, 0)
                    pool.wait_ge(deg_steps, cnt(b, 4, 3))
                    pw(dpow[:, :], dsafe[:, :], 2 * NB).then_inc(deg_pow, 1)

            def phase_r(b, p, c):
                if b is not None:
                    rstd_of("ln2b", b, 0)
                if c is not None:
                    rstd_of("ln1", c, 1)
                if b is not None:
                    rstd_of("ln2a", b, 1)
                    rstd_of("ln2b", b, 1)
                if c is not None:
                    for j in range(RS, NB - 2):
                        add_rows(c, j)
                    plus_b2(c)

            def plus_b2(c):
                pool.wait_ge(relu_done["ln1"], cnt(c, 2, 2))
                gp.tensor_tensor(by_block(xcols(c, 0, NB)), by_block(xcols(c, 0, NB)), over_blocks(b2bc, NB), ALU.add
                                 ).then_inc(xb2, 1)

            pool.wait_ge(const_ready, 1)
            pool.wait_ge(s0_dve, 5)
            pw(rs0[:, :], ve0[:, :], T0).then_inc(s0_pool, 1)
            pool.wait_ge(s0_dve, 6)
            pw(dg0[:, 3, :], dg0[:, 2, :], T0 * G0).then_inc(s0_pool, 1)
            add_rows(0, 1)
            rstd_of("ln1", 0, 0)
            rstd_of("ln1", 0, 1)
            for j in range(2, NB):
                add_rows(0, j)
            pool.wait_ge(first_steps, 3)
            pw(rstd["ln1"][0][:, 0:1], veps["ln1"][0][:, 0:1], 1).then_inc(first_pow, 1)
            pool.wait_ge(first_pow, 1)
            gp.tensor_tensor(shift["ln1"][0][:, 0:1], negmean["ln1"][0][:, 0:1], rstd["ln1"][0][:, 0:1], ALU.mult
                             ).then_inc(first_rstd, 1)
            pool.wait_ge(first_relu, 1)
            pool.wait_ge(w_in, 16 * 5)
            plus_b2(0)
            phase_p(0, None, 1)
            phase_q(0, None, 1)
            phase_r(0, None, 1)
            with pool.Fori(1, B - 1) as i:
                phase_p(i, i - 1, i + 1)
                phase_q(i, i - 1, i + 1)
                phase_r(i, i - 1, i + 1)
            phase_p(B - 1, B - 2, None)
            phase_q(B - 1, B - 2, None)
            phase_r(B - 1, B - 2, None)
            phase_p(None, B - 1, None)


def kernel(**inputs):
    import concourse.bacc as bacc
    from concourse.bass_utils import run_bass_kernel_spmd as run

    def laid(a):
        return np.ascontiguousarray(a)

    x, adj = np.asarray(inputs["x"]), np.asarray(inputs["adj"])
    node = np.arange(P) % S0
    member = np.stack([np.isin(node, g) for g in GROUPS], 1).astype(np.float32)
    corners = np.zeros((P, T0, P), np.float32)
    for g in range(B):
        t, q = divmod(g, P // S0)
        corners[q * S0:(q + 1) * S0, t, q * S0:(q + 1) * S0] = adj[g, 0:S0, 0:S0].T
    w20 = np.asarray(inputs["L0_gnn_W2"]).reshape(G0, 2, P, D).transpose(2, 0, 1, 3).reshape(P, G0 * 2 * D)
    w10 = np.asarray(inputs["L0_gnn_W1"]).transpose(1, 0, 2).reshape(P, G0 * E0)
    w2 = np.asarray(inputs["L1_gnn_W2"]).reshape(KH, P, D).transpose(1, 0, 2).reshape(P, KH * D)
    arrays = {
        "x": x,
        "adjT": adj.transpose(0, 2, 1),
        "in0": np.concatenate([x[:, 0:S0].reshape(T0, P, D).transpose(1, 0, 2).reshape(P, T0 * D),
                               corners.reshape(P, T0 * P), member], 1),
        "ident": np.eye(P, dtype=np.float32),
        "w0": np.concatenate([w10, w20], 1),
        "b0": np.concatenate([np.asarray(inputs[f"L0_gnn_b{k}"]).reshape(-1) for k in (1, 2)]),
        "weights": np.concatenate([w2, np.asarray(inputs["L2_gnn_W_neigh"]),
                                   np.asarray(inputs["L3_gnn_W"]).T], 1),
        "rows": np.concatenate([np.asarray(inputs[name]).reshape(-1) for name in (
            "L1_gnn_rms_weight", "L1_gnn_b2", "L2_gnn_gamma", "L2_gnn_beta", "L3_gnn_b", "L1_gnn_epsilon")]),
    }
    for name in ("L0_gnn_fusion_w", "L1_gnn_b1", "L1_gnn_W1", "L2_gnn_W_self"):
        arrays[name] = np.asarray(inputs[name])
    nc = bacc.Bacc("TRN2", target_bir_lowering=False, num_devices=1, dynamic_dma_scratch_size=1024)
    arrays = {f"in_{k}": laid(a) for k, a in arrays.items()}
    t_in = {k[3:]: nc.dram_tensor(k, a.shape, F32, kind="ExternalInput").ap() for k, a in arrays.items()}
    out = nc.dram_tensor("out", x.shape, F32, kind="ExternalOutput").ap()
    build(nc, t_in, out)
    return run(nc, [arrays], core_ids=[0]).results[0]["out"]
```
